# Optimizing a Trainium2 kernel written in Bass

```python
import numpy as np
import jax
import jax.numpy as jnp

def _softmax(x, axis=-1):
    return jax.nn.softmax(x, axis=axis)

def _gelu(x):
    return jax.nn.gelu(x, approximate=True)

def _silu(x):
    return jax.nn.silu(x)

def _sigmoid(x):
    return jax.nn.sigmoid(x)

def _layernorm(x, axis=-1, eps=1e-05):
    m = jnp.mean(x, axis=axis, keepdims=True)
    v = jnp.var(x, axis=axis, keepdims=True)
    return (x - m) / jnp.sqrt(v + eps)

def _scatter_add(tgt, idx, src, axis=0):
    return tgt.at[idx].add(src)

def _segment_sum(src, seg, n):
    return jax.ops.segment_sum(src, seg, n)
kernel_name = 'mk_xattn_ffn_d1_seqx_r2_35e146'

def setup_inputs(seed: int=0):
    np.random.seed(seed)
    _w = jnp.asarray

    def _rec_inputs():
        import jax
        import jax.numpy as jnp
        _rk = jax.random.key(seed)
        x = 7.22e-05 + 1 * jax.random.normal(jax.random.fold_in(_rk, 1), (32, 512, 512), jnp.float32)
        _lenS = 512 - jax.random.randint(jax.random.fold_in(_rk, 7), (32,), 0, max(1, 512 // 4) + 1, jnp.int32)
        _lenS2 = 512 - jax.random.randint(jax.random.fold_in(_rk, 8), (32,), 0, max(1, 512 // 4) + 1, jnp.int32)
        _ctx_1024P = jax.random.normal(jax.random.fold_in(_rk, 11), (32, 16, 512), jnp.float32)
        _ctx_1024c = jax.random.dirichlet(jax.random.fold_in(_rk, 511), 0.3 * jnp.ones((16,), jnp.float32), (32, 512))
        _ctx_1024t = jnp.einsum('bsk,bkd->bsd', _ctx_1024c, _ctx_1024P)
        _ctx_1024t = _ctx_1024t * jax.lax.rsqrt(jnp.mean(jnp.square(_ctx_1024t)) + 1e-12) * 0.953939
        ctx_1024 = 4.13588e-05 + 0.999923 * (_ctx_1024t + 0.3 * jax.random.normal(jax.random.fold_in(_rk, 611), (32, 512, 512), jnp.float32))
        return (x, ctx_1024)
    x, ctx_1024 = _rec_inputs()

    def _L0_xattn_setup():
        import jax, jax.numpy as jnp
        import numpy as np
        HEADS = 16
        D_MODEL = 512
        D_K = D_MODEL // HEADS
        key = jax.random.key(seed)
        ks = jax.random.split(key, 11)
        B, S = (4, 1024)
        scale = 1.0 / np.sqrt(D_MODEL)
        inp = {'query': jax.random.normal(ks[0], (B, S, D_MODEL), dtype=jnp.float32), 'key': jax.random.normal(ks[1], (B, S, D_MODEL), dtype=jnp.float32), 'value': jax.random.normal(ks[2], (B, S, D_MODEL), dtype=jnp.float32), 'Wq': jax.random.normal(ks[3], (D_MODEL, D_MODEL), dtype=jnp.float32) * scale, 'bq': jnp.zeros((D_MODEL,), dtype=jnp.float32), 'Wk': jax.random.normal(ks[4], (D_MODEL, D_MODEL), dtype=jnp.float32) * scale, 'bk': jnp.zeros((D_MODEL,), dtype=jnp.float32), 'Wv': jax.random.normal(ks[5], (D_MODEL, D_MODEL), dtype=jnp.float32) * scale, 'bv': jnp.zeros((D_MODEL,), dtype=jnp.float32), 'Wo': jax.random.normal(ks[6], (D_MODEL, D_MODEL), dtype=jnp.float32) * scale, 'bo': jnp.zeros((D_MODEL,), dtype=jnp.float32)}
        return inp
    _L0_xattn_all = _L0_xattn_setup()
    _L0_xattn_in = {k: v for k, v in _L0_xattn_all.items() if k in ('Wq', 'bq', 'Wk', 'bk', 'Wv', 'bv', 'Wo', 'bo')}
    del _L0_xattn_all

    def _L0_ffn_setup():
        import jax, jax.numpy as jnp
        import numpy as np
        E = 8
        K = 2
        R = 64
        ALPHA = 128.0
        SCALING = ALPHA / R
        key = jax.random.key(seed)
        k0, k1, k2, k3 = jax.random.split(key, 4)
        B, S, D = (4, 2048, 512)
        x = jax.random.normal(k0, (B, S, D), jnp.float32)
        Wg = jax.random.normal(k1, (E, D), jnp.float32) * 0.02
        bg = jnp.zeros((E,), jnp.float32)
        W1 = jax.random.normal(k2, (E, R, D), jnp.float32) * (1.0 / np.sqrt(D))
        W2 = jax.random.normal(k3, (E, D, R), jnp.float32) * 0.02
        return {'x': x, 'Wg': Wg, 'bg': bg, 'W1': W1, 'W2': W2}
    _L0_ffn_all = _L0_ffn_setup()
    _L0_ffn_in = {k: v for k, v in _L0_ffn_all.items() if k in ('Wg', 'bg', 'W1', 'W2')}
    del _L0_ffn_all
    return {'x': x, 'ctx_1024': ctx_1024, 'L0_xattn_Wq': _L0_xattn_in['Wq'], 'L0_xattn_bq': _L0_xattn_in['bq'], 'L0_xattn_Wk': _L0_xattn_in['Wk'], 'L0_xattn_bk': _L0_xattn_in['bk'], 'L0_xattn_Wv': _L0_xattn_in['Wv'], 'L0_xattn_bv': _L0_xattn_in['bv'], 'L0_xattn_Wo': _L0_xattn_in['Wo'], 'L0_xattn_bo': _L0_xattn_in['bo'], 'L0_ffn_Wg': _L0_ffn_in['Wg'], 'L0_ffn_bg': _L0_ffn_in['bg'], 'L0_ffn_W1': _L0_ffn_in['W1'], 'L0_ffn_W2': _L0_ffn_in['W2']}

def reference(x, ctx_1024, L0_xattn_Wq, L0_xattn_bq, L0_xattn_Wk, L0_xattn_bk, L0_xattn_Wv, L0_xattn_bv, L0_xattn_Wo, L0_xattn_bo, L0_ffn_Wg, L0_ffn_bg, L0_ffn_W1, L0_ffn_W2):
    import jax
    import jax.numpy as jnp

    def _L0_xattn_ref(query, key, value, Wq, bq, Wk, bk, Wv, bv, Wo, bo):
        import jax, jax.numpy as jnp
        import numpy as np
        HEADS = 16
        D_MODEL = 512
        D_K = D_MODEL // HEADS
        B, S, _ = query.shape

        def proj(x, W, b):
            y = x @ W.T + b
            return y.reshape(B, S, HEADS, D_K).transpose(0, 2, 1, 3)
        q = proj(query, Wq, bq)
        k = proj(key, Wk, bk)
        v = proj(value, Wv, bv)
        scores = jnp.einsum('bhqd,bhkd->bhqk', q, k) / jnp.sqrt(jnp.float32(D_K))
        p_attn = jax.nn.softmax(scores, axis=-1)
        x = jnp.einsum('bhqk,bhkd->bhqd', p_attn, v)
        x = x.transpose(0, 2, 1, 3).reshape(B, S, HEADS * D_K)
        return x @ Wo.T + bo

    def _L0_ffn_ref(x, Wg, bg, W1, W2):
        import jax, jax.numpy as jnp
        import numpy as np
        E = 8
        K = 2
        R = 64
        ALPHA = 128.0
        SCALING = ALPHA / R
        orig_shape = x.shape
        D = orig_shape[-1]
        xf = x.reshape(-1, D)
        logits = xf @ Wg.T + bg
        top_gates, top_idx = jax.lax.top_k(logits, K)
        top_gates = jax.nn.softmax(top_gates, axis=-1)
        h = jax.nn.gelu(jnp.einsum('nd,erd->enr', xf, W1), approximate=False)
        eout = SCALING * jnp.einsum('enr,edr->ned', h, W2)
        sel = jnp.take_along_axis(eout, top_idx[:, :, None], axis=1)
        out = jnp.sum(top_gates[:, :, None] * sel, axis=1)
        return out.reshape(orig_shape)
    x = x + _L0_xattn_ref(_layernorm(x, axis=-1), ctx_1024, ctx_1024, L0_xattn_Wq, L0_xattn_bq, L0_xattn_Wk, L0_xattn_bk, L0_xattn_Wv, L0_xattn_bv, L0_xattn_Wo, L0_xattn_bo)
    x = x + _L0_ffn_ref(_layernorm(x, axis=-1), L0_ffn_Wg, L0_ffn_bg, L0_ffn_W1, L0_ffn_W2)
    return x

_drawn_inputs = setup_inputs


def setup_inputs(seed=0):
    import zlib

    import numpy as np

    out = dict(_drawn_inputs(seed))
    spreads = {'L0_xattn_bq': (0.0, 0.327),
     'L0_xattn_bk': (0.0, 0.8),
     'L0_xattn_bv': (0.0, 0.1),
     'L0_xattn_bo': (0.0, 0.1),
     'L0_ffn_bg': (0.0, 0.1)}
    factors = {}
    for name, (base, spread) in spreads.items():
        noise = np.random.default_rng([zlib.crc32(name.encode()), seed]).standard_normal(out[name].shape)
        drawn = base * np.exp(spread * noise) if base else spread * noise
        out[name] = jnp.asarray(drawn.astype(out[name].dtype))
    for name, factor in factors.items():
        out[name] = (out[name] * factor).astype(out[name].dtype)
    return out
```

```python
from contextlib import ExitStack

import concourse.bass as bass
from concourse import mybir
import numpy as np

F32 = mybir.dt.float32
F16 = mybir.dt.float16
ALU = mybir.AluOpType
ACT = mybir.ActivationFunctionType
AX_X = mybir.AxisListType.X

P = 128
HEADS = 16
DK = 32
EXPERTS = 8
LN_EPS = 1e-5
SCALE_W = 64.0
MAX_UNIT = SCALE_W * SCALE_W
SCALING = 2.0
DMA = 16


class Count:

    def __init__(self, sem, per):
        self.sem, self.per = sem, per

    def at(self, b, n):
        return b * self.per + n


def xattn_moe_kernel(nc, x, ctx, wq_t, bq, wk_t, bk, wv_t, bv, wo_t, bo, wg_t, bg, w1_t, w2_t,
                     ident, select, lower, out):
    B, T, D = x.shape
    TT = T // P
    DT = D // P
    HT = P // DK
    GROUPS = HEADS // HT
    EXP_SCALE = 1.0 / (MAX_UNIT * float(np.sqrt(np.float32(DK))))
    UNW = 1.0 / SCALE_W
    STACK = 3 * DK
    MAX_UNITS = HEADS * TT // 2
    RING = 3
    LN_STEPS = 8

    with ExitStack() as st:
        def sb(name, shape, dt):
            return st.enter_context(nc.sbuf_tensor(name, shape, dt))

        def pb(name, shape, dt):
            return st.enter_context(nc.psum_tensor(name, shape, dt))

        def count(name, per):
            return Count(st.enter_context(nc.semaphore(name)), per)

        w_hi = {n: sb(f"w{n}_hi", [P, DT, D], F16) for n in ("q", "k", "v", "o", "1", "2")}
        w_lo = {n: sb(f"w{n}_lo", [P, DT, D], F16) for n in ("q", "k", "v", "o", "1", "2")}
        wg_hi = sb("wg_hi", [P, DT, EXPERTS], F16)
        wg_lo = sb("wg_lo", [P, DT, EXPERTS], F16)
        bq_col = sb("bq_col", [P, DT], F32)
        bk_col = sb("bk_col", [P, DT], F32)
        bv_row = sb("bv_row", [P, D], F32)
        bo_row = sb("bo_row", [P, D], F32)
        bg_row = sb("bg_row", [P, EXPERTS], F32)
        ident32 = sb("ident32", [P, P], F32)
        ident16 = sb("ident16", [P, P], F16)
        select16 = sb("select16", [2 * EXPERTS, DT, P], F16)
        lower_tri = sb("lower_tri", [P, EXPERTS, EXPERTS], F32)
        ones = sb("ones", [P, DK], F32)
        minus_half = sb("minus_half", [P, TT], F32)
        three_halves = sb("three_halves", [P, TT], F32)

        x_buf = [sb(f"x_buf{p}", [P, TT, D], F32) for p in range(2)]
        ctx_buf = sb("ctx_buf", [P, TT, D], F32)
        xn = sb("xn", [P, 2, D], F32)
        ctxT_hi = sb("ctxT_hi", [P, DT, T], F16)
        ctxT_lo = sb("ctxT_lo", [P, DT, T], F16)
        xT_hi = sb("xT_hi", [P, DT, T], F16)
        xT_lo = sb("xT_lo", [P, DT, T], F16)
        q_hi = sb("q_hi", [P, DT, T], F16)
        q_lo = sb("q_lo", [P, DT, T], F16)
        k_hi = sb("k_hi", [P, DT, T], F16)
        k_lo = sb("k_lo", [P, DT, T], F16)
        q_stack = sb("q_stack", [P, HEADS, T], F16)
        k_stack = sb("k_stack", [P, HEADS, T], F16)
        v_buf = [sb(f"v_buf{p}", [P, TT, D], F32) for p in range(2)]
        shared = sb("shared", [P, (RING + 1) * HT * T], F32)
        probs = [shared[:, s * HT * T:(s + 1) * HT * T].rearrange("p (j q) -> p j q", j=HT)
                 for s in range(RING)]
        prob_sum = shared[:, RING * HT * T:(RING + 1) * HT * T].rearrange("p (j q) -> p j q", j=HT)
        h_buf = probs[0]
        gh_hi = shared[:, HT * T:HT * T + HT * T // 2].bitcast(F16).rearrange("p (j q) -> p j q", j=HT)
        gh_lo = shared[:, HT * T + HT * T // 2:2 * HT * T].bitcast(F16).rearrange("p (j q) -> p j q", j=HT)
        gh32 = probs[2][:, 0:2, :]
        x1T32 = probs[2][:, 2:4, :]
        cmp_gt = prob_sum[:, 0, 0:TT * EXPERTS * EXPERTS].rearrange("p (t e j) -> p t e j", t=TT, e=EXPERTS)
        cmp_eq = prob_sum[:, 1, 0:TT * EXPERTS * EXPERTS].rearrange("p (t e j) -> p t e j", t=TT, e=EXPERTS)
        stage = [shared[:, n * DT * D:(n + 1) * DT * D].rearrange("p (t d) -> p t d", t=DT) for n in range(2)]

        o_buf = sb("o_buf", [P, T], F32)
        inv_den = sb("inv_den", [P, T], F32)
        o_hi = sb("o_hi", [P, DT, T], F16)
        o_lo = sb("o_lo", [P, DT, T], F16)
        maxima = sb("maxima", [P, HEADS * TT], F32)
        neg_max = sb("neg_max", [P, HEADS * TT], F16)
        max_rows = sb("max_rows", [HEADS * TT // 2, 2, P], F16)
        stats = sb("stats", [P, TT, 6], F32)
        moment_tmp = sb("moment_tmp", [P, 4, TT], F32)
        ln_tmp = sb("ln_tmp", [P, 8, TT], F32)
        logits = sb("logits", [P, TT, EXPERTS], F32)
        top1 = sb("top1", [P, TT], F32)
        rank = sb("rank", [P, TT, EXPERTS], F32)
        gap = sb("gap", [P, TT, EXPERTS], F32)
        gate_exp = sb("gate_exp", [P, TT, EXPERTS], F32)
        gate_den = sb("gate_den", [P, 2, TT], F32)
        gates = sb("gates", [P, TT, EXPERTS], F32)
        gate_pair = sb("gate_pair", [P, TT, 2 * EXPERTS], F16)
        gateT = sb("gateT", [2 * EXPERTS, T], F16)

        scores = [pb(f"scores{n}", [P, 2, T], F32) for n in range(2)]
        work = [pb(f"work{n}", [P, T], F32) for n in range(4)]
        oT, den = work[2], work[3]

        const_in = count("const_in", 0)
        stage_in = [count(f"stage_in{n}", 0) for n in range(2)]
        ln_const = count("ln_const", 0)
        setup_hi = count("setup_hi", 0)
        setup_lo = count("setup_lo", 0)
        x_in = count("x_in", DMA)
        ctx_in = count("ctx_in", DMA)
        stack_in = [count(f"stack_in{n}", 24 * DMA) for n in range(2)]
        maxrow_in = [count(f"maxrow_in{n}", DMA) for n in range(2)]
        out_stored = count("out_stored", TT * DMA)
        stats1 = count("stats1", TT)
        MOMENTS = 6
        moments1 = count("moments1", MOMENTS)
        ln1_step = count("ln1_step", LN_STEPS)
        xn_ready = count("xn_ready", TT)
        xbo_ready = count("xbo_ready", TT)
        ctxT_ps = count("ctxT_ps", TT)
        ctxT_hi_s = count("ctxT_hi_s", TT)
        ctxT_lo_s = count("ctxT_lo_s", TT)
        xT_ps = count("xT_ps", TT)
        xT_hi_s = count("xT_hi_s", TT)
        xT_lo_s = count("xT_lo_s", TT)
        q_ps = count("q_ps", DT)
        q_hi_s = count("q_hi_s", DT)
        q_lo_s = count("q_lo_s", DT)
        k_ps = count("k_ps", DT)
        k_hi_s = count("k_hi_s", DT)
        k_lo_s = count("k_lo_s", DT)
        v_ps = count("v_ps", TT)
        v_ready = count("v_ready", TT)
        max_ps = count("max_ps", MAX_UNITS)
        max_done = count("max_done", MAX_UNITS)
        negmax_s = count("negmax_s", 2)
        maxT_ps = count("maxT_ps", 2)
        maxrow_s = count("maxrow_s", 2)
        STEPS = GROUPS * TT
        score_ps = count("score_ps", 2 * STEPS)
        exp_done = count("exp_done", 2 * STEPS)
        pv_done = count("pv_done", STEPS)
        sum_first = count("sum_first", GROUPS)
        sum_more = count("sum_more", 2 * GROUPS)
        den_ps = count("den_ps", GROUPS)
        o_copied = count("o_copied", GROUPS)
        inv_ready = count("inv_ready", GROUPS)
        o_scaled = count("o_scaled", GROUPS)
        o_hi_s = count("o_hi_s", GROUPS)
        o_lo_s = count("o_lo_s", GROUPS)
        op_ps = count("op_ps", TT)
        x1_ready = count("x1_ready", TT)
        stats2 = count("stats2", TT)
        moments2 = count("moments2", MOMENTS * TT)
        ln2_step = count("ln2_step", LN_STEPS * TT)
        x1n_ready = count("x1n_ready", TT)
        x1T_ps = count("x1T_ps", TT)
        x1T_hi_s = count("x1T_hi_s", TT)
        x1T_copied = count("x1T_copied", TT)
        x1T_lo_s = count("x1T_lo_s", TT)
        logit_ps = count("logit_ps", 1)
        GATE_A, GATE_B = 8, 6
        gate_a = count("gate_a", GATE_A)
        gate_exp_s = count("gate_exp_s", 1)
        gate_b = count("gate_b", GATE_B)
        gateT_ps = count("gateT_ps", 1)
        gateT_s = count("gateT_s", 1)
        w1_ps = count("w1_ps", DT)
        h_ready = count("h_ready", DT)
        gbc_ps = count("gbc_ps", DT)
        gh32_s = count("gh32_s", DT)
        gh_hi_s = count("gh_hi_s", DT)
        gh_lo_s = count("gh_lo_s", DT)
        w2_ps = count("w2_ps", TT)
        out_ready = count("out_ready", TT)

        bank_read = {"CT": ctxT_lo_s, "XT": xT_lo_s, "Q": q_lo_s, "K": k_lo_s, "V": v_ready,
                     "MT": maxrow_s, "OP": x1_ready, "T": x1T_copied, "LG": gate_a, "W1": h_ready,
                     "GT": gateT_s, "GB": gh32_s, "W2": out_ready, "O": o_copied, "DEN": inv_ready}

        A_AT = [[("CT", 0), ("CT", 1)], [("CT", 2), ("CT", 3)], [("K", 0)], [("K", 1)], [("K", 2)],
                [("K", 3)], [("XT", 0), ("XT", 1)], [("XT", 2), ("XT", 3)], [("Q", 0)], [("Q", 1)],
                [("Q", 2)], [("Q", 3)], [("V", 0)], [("V", 1)], [("V", 2)], []]
        A_TAIL = [("V", 3)]
        XN_AT = 5
        A_ORDER = [u for step in A_AT for u in step] + A_TAIL
        PHASE2 = ("B B B B OP0 B B OP1 B B OP2 T0 B B OP3 T1 B B T2 B B T3 B B LG0 MT0 W1_0 B B W1_1 B B "
                  "GT0 W1_2 B B W1_3 B B GB0 GB1 GB2 GB3 B B W2_0 B B W2_1 B B W2_2 B B MT1 W2_3").split()

        def phase2(with_d, with_b):
            steps, units = [], 0
            for s in PHASE2:
                kind, n = (s.split("_") if "_" in s else (s.rstrip("0123456789"), s[-1]))
                if kind == "B":
                    if with_b:
                        steps.append(("B", units))
                    units += 1
                elif with_b if kind == "MT" else with_d:
                    steps.append((kind, int(n)))
            assert units == MAX_UNITS
            return steps

        def banks(uses, count_of_banks):
            return {u: n % count_of_banks for n, u in enumerate(uses)}

        def d_uses(with_d, with_b):
            return [u for u in phase2(with_d, with_b) if u[0] != "B"]

        BANK_A = banks(A_ORDER, 2)

        def prior_uses(uses, bank_of, before):
            last, prior = dict(before), {}
            for kind, n, offset in uses:
                prior[kind, n] = last.get(bank_of[kind, n])
                last[bank_of[kind, n]] = (kind, n, offset)
            return prior, last

        def bank_tables(with_d, with_b, before):
            first, last = {}, dict(before)
            if with_b:
                first, last = prior_uses([(k, n, 1) for k, n in A_ORDER], BANK_A, last)
            if with_d:
                oT_prior, den_prior = last.get(2), last.get(3)
                last[2], last[3] = ("O", GROUPS - 1, 0), ("DEN", GROUPS - 1, 0)
            else:
                oT_prior = den_prior = None
            uses = d_uses(with_d, with_b)
            bank_of = banks(uses, 4)
            second, last = prior_uses([(k, n, 1 if k == "MT" else 0) for k, n in uses], bank_of, last)
            return first, (oT_prior, den_prior), bank_of, second, last

        def shifted(last):
            return {bank: (k, n, offset - 1) for bank, (k, n, offset) in last.items()}

        PROLOGUE = bank_tables(False, True, {})
        FIRST = bank_tables(True, True, shifted(PROLOGUE[4]))
        MIDDLE = bank_tables(True, True, shifted(FIRST[4]))
        assert shifted(MIDDLE[4]) == shifted(FIRST[4])
        LAST = bank_tables(True, False, shifted(MIDDLE[4]))

        def run_steps(engine, step):
            step(-1, 1, PROLOGUE, False, True)
            step(0, 0, FIRST, True, True)
            with engine.Fori(1, B - 3, 2) as i:
                step(i, 1, MIDDLE, True, True)
                step(i + 1, 0, MIDDLE, True, True)
            step(B - 3, 1, MIDDLE, True, True)
            step(B - 2, 0, MIDDLE, True, True)
            step(B - 1, 1, LAST, True, False)

        x_tiles = x.rearrange("b (t p) d -> b p t d", p=P)
        ctx_tiles = ctx.rearrange("b (t p) d -> b p t d", p=P)
        out_tiles = out.rearrange("b (t p) d -> b t p d", p=P)
        weights = [("q", wq_t), ("k", wk_t), ("v", wv_t), ("o", wo_t), ("1", w1_t), ("2", w2_t)]

        block = st.enter_context(nc.Block())

        @block.sync
        def _(sp):
            def stack(b, half, hi, lo, hi_s, lo_s, dst, order):
                sp.wait_ge(hi_s.sem, hi_s.at(b, 2 * half + 2))
                sp.wait_ge(lo_s.sem, lo_s.at(b, 2 * half + 2))
                for g, part in enumerate(order):
                    src = hi if part == "hi" else lo
                    for j in range(HT):
                        heads = dst[DK * g:DK * g + DK, :, :].rearrange("p (t j) q -> p t j q", j=HT)
                        sp.dma_start(heads[:, 2 * half:2 * half + 2, j, :],
                                     src[DK * j:DK * j + DK, 2 * half:2 * half + 2, :])\
                          .then_inc(stack_in[half].sem, DMA)

            def step(i, par, tables, with_d, with_b):
                if with_d and with_b:
                    if not (isinstance(i, int) and i == 0):
                        sp.wait_ge(out_stored.sem, out_stored.at(i - 1, TT * DMA))
                    sp.dma_start(x_buf[1 - par][:, :, :], x_tiles[i + 1]).then_inc(x_in.sem, DMA)
                if with_b:
                    for half in range(2):
                        if with_d:
                            sp.wait_ge(score_ps.sem, score_ps.at(i, STEPS * (half + 1)))
                        stack(i + 1, half, k_hi, k_lo, k_hi_s, k_lo_s, k_stack, ("hi", "lo", "hi"))
                        stack(i + 1, half, q_hi, q_lo, q_hi_s, q_lo_s, q_stack, ("hi", "hi", "lo"))
                        if half == 0 and not (isinstance(i, int) and i + 2 >= B):
                            sp.wait_ge(ctxT_ps.sem, ctxT_ps.at(i + 1, TT))
                            sp.dma_start(ctx_buf[:, :, :], ctx_tiles[i + 2]).then_inc(ctx_in.sem, DMA)
                for kind, n in phase2(with_d, with_b):
                    if kind == "MT":
                        sp.wait_ge(maxrow_s.sem, maxrow_s.at(i + 1, n + 1))
                        half_heads = HEADS // 2
                        sp.dma_start(
                            q_stack[STACK:STACK + 1, half_heads * n:half_heads * (n + 1), :],
                            max_rows[:, n, :]).then_inc(maxrow_in[n].sem, DMA)
                    if kind == "W2":
                        sp.wait_ge(out_ready.sem, out_ready.at(i, n + 1))
                        sp.dma_start(out_tiles[i, n], x_buf[par][:, n, :]).then_inc(out_stored.sem, DMA)

            sp.dma_start(ctx_buf[:, :, :], ctx_tiles[0]).then_inc(ctx_in.sem, DMA)
            sp.dma_start(x_buf[0][:, :, :], x_tiles[0]).then_inc(x_in.sem, DMA)
            sp.dma_start(ident32[:, :], ident).then_inc(const_in.sem, DMA)
            sp.dma_start(bq_col[:, :], bq).then_inc(const_in.sem, DMA)
            sp.dma_start(bk_col[:, :], bk).then_inc(const_in.sem, DMA)
            sp.dma_start(bv_row[:, :], bv.partition_broadcast(P)).then_inc(const_in.sem, DMA)
            sp.dma_start(bo_row[:, :], bo.partition_broadcast(P)).then_inc(const_in.sem, DMA)
            sp.dma_start(bg_row[:, :], bg.partition_broadcast(P)).then_inc(const_in.sem, DMA)
            sp.dma_start(lower_tri[:, :, :], lower.partition_broadcast(P)).then_inc(const_in.sem, DMA)
            sp.dma_start(o_buf[:, 0:DT * EXPERTS].rearrange("p (t e) -> p t e", t=DT),
                         wg_t.rearrange("(t p) e -> p t e", p=P))\
              .then_inc(const_in.sem, DMA)
            sp.dma_start(inv_den[0:2 * EXPERTS, :], select).then_inc(const_in.sem, DMA)
            for n, (_, w) in enumerate(weights):
                if n >= 2:
                    sp.wait_ge(setup_lo.sem, n - 1)
                sp.dma_start(stage[n % 2], w.rearrange("(t p) d -> p t d", p=P)).then_inc(stage_in[n % 2].sem, DMA)
            run_steps(sp, step)
            sp.wait_ge(out_stored.sem, out_stored.at(B, 0))

        @block.gpsimd
        def _(pool):
            pool.memset(minus_half[:, :], -0.5).then_inc(ln_const.sem, 1)
            pool.memset(three_halves[:, :], 1.5).then_inc(ln_const.sem, 1)

            def inv_std(b, tiles, base, step_s):
                c = slice(tiles[0], tiles[-1] + 1)
                mean2, var, first, sq, half, factor, inv, neg = (ln_tmp[:, n, c] for n in range(8))
                mh, th = minus_half[:, c], three_halves[:, c]
                for n, (dst, lhs, rhs, op) in enumerate([
                        (first, var, mh, ALU.pow), (sq, first, first, ALU.mult), (half, sq, var, ALU.mult),
                        (half, half, mh, ALU.mult), (factor, half, th, ALU.add), (inv, first, factor, ALU.mult),
                        (neg, mean2, inv, ALU.mult), (neg, neg, mh, ALU.mult)]):
                    if n:
                        pool.wait_ge(step_s.sem, step_s.at(b, base + n))
                    pool.tensor_tensor(dst, lhs, rhs, op).then_inc(step_s.sem, 1)

            def add_bo(b, par):
                pool.wait_ge(xn_ready.sem, xn_ready.at(b, TT))
                for t in range(TT):
                    pool.tensor_tensor(x_buf[par][:, t, :], x_buf[par][:, t, :], bo_row[:, :], ALU.add)\
                        .then_inc(xbo_ready.sem, 1)

            def step(i, par, tables, with_d, with_b):
                if with_b:
                    pool.wait_ge(moments1.sem, moments1.at(i + 1, MOMENTS))
                    inv_std(i + 1, range(TT), 0, ln1_step)
                for s in range(STEPS):
                    if with_d and s % TT == 1:
                        g = s // TT
                        pool.wait_ge(exp_done.sem, exp_done.at(i, 2 * s + 2))
                        if g >= 1:
                            pool.wait_ge(den_ps.sem, den_ps.at(i, g))
                        pool.tensor_tensor(prob_sum[:, :, :], probs[(s - 1) % RING], probs[s % RING], ALU.add)\
                            .then_inc(sum_first.sem, 1)
                    if with_d and s >= 6 and (s - 6) % TT == 0:
                        o_low(i, (s - 6) // TT)
                    if with_b and s == 7:
                        add_bo(i + 1, 1 - par)
                if with_d:
                    o_low(i, GROUPS - 1)
                for kind, n in phase2(with_d, with_b):
                    if kind == "OP":
                        pool.wait_ge(moments2.sem, moments2.at(i, MOMENTS * (n + 1)))
                        inv_std(i, range(n, n + 1), LN_STEPS * n, ln2_step)
                    if kind == "T":
                        pool.wait_ge(x1T_hi_s.sem, x1T_hi_s.at(i, n + 1))
                        pool.wait_ge(x1T_copied.sem, x1T_copied.at(i, n + 1))
                        cols = slice(P * n, P * n + P)
                        pool.tensor_tensor(xT_lo[:, :, cols],
                                           x1T32[:, n % 2, :].rearrange("p (t c) -> p t c", t=DT),
                                           xT_hi[:, :, cols], ALU.subtract).then_inc(x1T_lo_s.sem, 1)
                    if kind == "GB":
                        pool.wait_ge(gh_hi_s.sem, gh_hi_s.at(i, n + 1))
                        pool.tensor_tensor(gh_lo[:, n, :], gh32[:, n % 2, :], gh_hi[:, n, :], ALU.subtract)\
                            .then_inc(gh_lo_s.sem, 1)

            def o_low(i, g):
                pool.wait_ge(o_hi_s.sem, o_hi_s.at(i, g + 1))
                pool.tensor_tensor(o_lo[:, g, :], o_buf[:, :], o_hi[:, g, :], ALU.subtract)\
                    .then_inc(o_lo_s.sem, 1)

            pool.wait_ge(ln_const.sem, 4)
            pool.wait_ge(const_in.sem, 9 * DMA)
            run_steps(pool, step)

        @block.scalar
        def _(act):
            for n, (name, _) in enumerate(weights):
                act.wait_ge(stage_in[n % 2].sem, DMA * (n // 2 + 1))
                act.activation(w_hi[name][:, :, :], stage[n % 2], ACT.Copy, scale=SCALE_W).then_inc(setup_hi.sem, 1)
            act.wait_ge(const_in.sem, 9 * DMA)
            act.activation(wg_hi[:, :, :], o_buf[:, 0:DT * EXPERTS].rearrange("p (t e) -> p t e", t=DT),
                           ACT.Copy, scale=SCALE_W).then_inc(setup_hi.sem, 1)
            act.activation(ident16[:, :], ident32[:, :], ACT.Copy).then_inc(setup_hi.sem, 1)
            act.activation(select16[:, :, :], inv_den[0:2 * EXPERTS, :].rearrange("p (t c) -> p t c", t=DT),
                           ACT.Copy).then_inc(setup_hi.sem, 1)
            act.wait_ge(setup_lo.sem, len(weights) + 3)

            def a_part(b, kind, n):
                cols = slice(P * n, P * n + P)
                bank = work[BANK_A[kind, n]]
                if kind == "CT":
                    act.wait_ge(ctxT_ps.sem, ctxT_ps.at(b, n + 1))
                    act.activation(ctxT_hi[:, :, cols], bank[:, :].rearrange("p (t c) -> p t c", t=DT), ACT.Copy)\
                       .then_inc(ctxT_hi_s.sem, 1)
                if kind == "XT":
                    act.wait_ge(xT_ps.sem, xT_ps.at(b, n + 1))
                    act.activation(xT_hi[:, :, cols], bank[:, :].rearrange("p (t c) -> p t c", t=DT), ACT.Copy)\
                       .then_inc(xT_hi_s.sem, 1)
                if kind == "Q":
                    act.wait_ge(q_ps.sem, q_ps.at(b, n + 1))
                    act.activation(q_hi[:, n, :], bank[:, :], ACT.Identity, bias=bq_col[:, n:n + 1])\
                       .then_inc(q_hi_s.sem, 1)
                if kind == "K":
                    act.wait_ge(k_ps.sem, k_ps.at(b, n + 1))
                    act.activation(k_hi[:, n, :], bank[:, :], ACT.Identity, bias=bk_col[:, n:n + 1])\
                       .then_inc(k_hi_s.sem, 1)

            def normalise(b, buf, t, step_s, steps, ps, ready):
                act.wait_ge(step_s.sem, step_s.at(b, steps))
                if t >= 2:
                    act.wait_ge(ps.sem, ps.at(b, t - 1))
                act.activation(xn[:, t % 2, :], buf[:, t, :], ACT.Identity, bias=ln_tmp[:, 7, t:t + 1],
                               scale=ln_tmp[:, 6, t:t + 1]).then_inc(ready.sem, 1)

            def step(i, par, tables, with_d, with_b):
                def copy_o(g):
                    act.wait_ge(pv_done.sem, pv_done.at(i, TT * (g + 1)))
                    if g >= 1:
                        act.wait_ge(o_lo_s.sem, o_lo_s.at(i, g))
                    act.activation(o_buf[:, :], oT[:, :], ACT.Copy).then_inc(o_copied.sem, 1)

                def o_high(g):
                    act.wait_ge(o_scaled.sem, o_scaled.at(i, g + 1))
                    act.activation(o_hi[:, g, :], o_buf[:, :], ACT.Copy).then_inc(o_hi_s.sem, 1)

                for s in range(STEPS):
                    if with_d:
                        for pr in range(2):
                            act.wait_ge(score_ps.sem, score_ps.at(i, 2 * s + pr + 1))
                            if s >= RING and pr == 0:
                                act.wait_ge(pv_done.sem, pv_done.at(i, s - RING + 1))
                                late = s - RING
                                if late % TT <= 1:
                                    act.wait_ge(sum_first.sem, sum_first.at(i, late // TT + 1))
                                else:
                                    act.wait_ge(sum_more.sem, sum_more.at(i, 2 * (late // TT) + late % TT - 1))
                            act.activation(probs[s % RING][:, 2 * pr:2 * pr + 2, :], scores[pr][:, :, :], ACT.Exp,
                                           scale=EXP_SCALE).then_inc(exp_done.sem, 1)
                    if with_b:
                        if s == XN_AT:
                            for t in range(2):
                                normalise(i + 1, x_buf[1 - par], t, ln1_step, LN_STEPS, xT_ps, xn_ready)
                        for kind, n in A_AT[s]:
                            a_part(i + 1, kind, n)
                            if kind == "XT" and n < 2:
                                normalise(i + 1, x_buf[1 - par], n + 2, ln1_step, LN_STEPS, xT_ps, xn_ready)
                    if with_d and s % TT == 0 and s >= TT:
                        copy_o(s // TT - 1)
                    if with_d and s >= 6 and (s - 6) % TT == 0:
                        o_high((s - 6) // TT)
                if with_d:
                    copy_o(GROUPS - 1)
                    o_high(GROUPS - 1)
                bank_of = tables[2]
                for kind, n in phase2(with_d, with_b):
                    bank = None if kind == "B" else work[bank_of[kind, n]]
                    cols = slice(P * n, P * n + P)
                    if kind == "OP":
                        normalise(i, x_buf[par], n, ln2_step, LN_STEPS * (n + 1), x1T_ps, x1n_ready)
                    if kind == "T":
                        act.wait_ge(x1T_ps.sem, x1T_ps.at(i, n + 1))
                        act.activation(xT_hi[:, :, cols], bank[:, :].rearrange("p (t c) -> p t c", t=DT), ACT.Copy)\
                           .then_inc(x1T_hi_s.sem, 1)
                        if n >= 2:
                            act.wait_ge(x1T_lo_s.sem, x1T_lo_s.at(i, n - 1))
                        act.activation(x1T32[:, n % 2, :], bank[:, :], ACT.Copy).then_inc(x1T_copied.sem, 1)
                    if kind == "MT":
                        act.wait_ge(maxT_ps.sem, maxT_ps.at(i + 1, n + 1))
                        act.activation(max_rows[:, n, :], bank[:, :].bitcast(F16)[0:HEADS * TT // 2, 0:P], ACT.Copy)\
                           .then_inc(maxrow_s.sem, 1)
                    if kind == "LG":
                        act.wait_ge(gate_a.sem, gate_a.at(i, GATE_A))
                        act.activation(gate_exp[:, :, :], gap[:, :, :], ACT.Exp).then_inc(gate_exp_s.sem, 1)
                    if kind == "W1":
                        act.wait_ge(w1_ps.sem, w1_ps.at(i, n + 1))
                        act.activation(h_buf[:, n, :], bank[:, :], ACT.Gelu, scale=UNW).then_inc(h_ready.sem, 1)
                    if kind == "GT":
                        act.wait_ge(gateT_ps.sem, gateT_ps.at(i, 1))
                        act.activation(gateT[:, :], bank[:, :].bitcast(F16)[0:2 * EXPERTS, 0:T], ACT.Copy)\
                           .then_inc(gateT_s.sem, 1)
                    if kind == "GB":
                        act.wait_ge(gh32_s.sem, gh32_s.at(i, n + 1))
                        act.activation(gh_hi[:, n, :], gh32[:, n % 2, :], ACT.Copy).then_inc(gh_hi_s.sem, 1)

            run_steps(act, step)

        @block.vector
        def _(dve):
            dve.memset(ones[:, :], 1.0).then_inc(ln_const.sem, 1)
            dve.memset(k_stack[STACK:STACK + 1, :, :], MAX_UNIT).then_inc(ln_const.sem, 1)
            for n, (name, _) in enumerate(weights):
                dve.wait_ge(setup_hi.sem, n + 1)
                dve.scalar_tensor_tensor(out=w_lo[name][:, :, :], in0=stage[n % 2], scalar=SCALE_W,
                                         in1=w_hi[name][:, :, :], op0=ALU.mult, op1=ALU.subtract)\
                   .then_inc(setup_lo.sem, 1)
            dve.wait_ge(setup_hi.sem, len(weights) + 1)
            dve.scalar_tensor_tensor(out=wg_lo[:, :, :],
                                     in0=o_buf[:, 0:DT * EXPERTS].rearrange("p (t e) -> p t e", t=DT),
                                     scalar=SCALE_W, in1=wg_hi[:, :, :], op0=ALU.mult, op1=ALU.subtract)\
               .then_inc(setup_lo.sem, 1)
            dve.tensor_scalar(bq_col[:, :], bq_col[:, :], SCALE_W, None, ALU.mult).then_inc(setup_lo.sem, 1)
            dve.tensor_scalar(bk_col[:, :], bk_col[:, :], SCALE_W, None, ALU.mult).then_inc(setup_lo.sem, 1)
            dve.wait_ge(setup_lo.sem, len(weights) + 3)

            def moments(tiles, stats_s, moment_s, b, base):
                c = slice(tiles[0], tiles[-1] + 1)
                mean_a, m2_a, mean_b, m2_b = (stats[:, c, n] for n in (1, 2, 4, 5))
                diff, m2, sq, quarter = (moment_tmp[:, n, c] for n in range(4))
                dve.wait_ge(stats_s.sem, stats_s.at(b, tiles[-1] + 1))
                dve.tensor_tensor(ln_tmp[:, 0, c], mean_a, mean_b, ALU.add).then_inc(moment_s.sem, 1)
                dve.tensor_tensor(diff, mean_a, mean_b, ALU.subtract).then_inc(moment_s.sem, 1)
                dve.tensor_tensor(m2, m2_a, m2_b, ALU.add).then_inc(moment_s.sem, 1)
                dve.wait_ge(moment_s.sem, moment_s.at(b, base + 2))
                dve.tensor_tensor(sq, diff, diff, ALU.mult).then_inc(moment_s.sem, 1)
                dve.wait_ge(moment_s.sem, moment_s.at(b, base + 4))
                dve.tensor_scalar(quarter, sq, 0.25, LN_EPS, ALU.mult, ALU.add).then_inc(moment_s.sem, 1)
                dve.wait_ge(moment_s.sem, moment_s.at(b, base + 5))
                dve.scalar_tensor_tensor(out=ln_tmp[:, 1, c], in0=m2, scalar=1.0 / D, in1=quarter,
                                         op0=ALU.mult, op1=ALU.add).then_inc(moment_s.sem, 1)

            def a_part(b, par, kind, n):
                cols = slice(P * n, P * n + P)
                bank = work[BANK_A[kind, n]]
                tiles = bank[:, :].rearrange("p (t c) -> p t c", t=DT)
                if kind == "CT":
                    dve.wait_ge(ctxT_hi_s.sem, ctxT_hi_s.at(b, n + 1))
                    dve.tensor_tensor(ctxT_lo[:, :, cols], tiles, ctxT_hi[:, :, cols], ALU.subtract)\
                       .then_inc(ctxT_lo_s.sem, 1)
                if kind == "XT":
                    dve.wait_ge(xT_hi_s.sem, xT_hi_s.at(b, n + 1))
                    dve.tensor_tensor(xT_lo[:, :, cols], tiles, xT_hi[:, :, cols], ALU.subtract)\
                       .then_inc(xT_lo_s.sem, 1)
                if kind == "Q":
                    dve.wait_ge(q_hi_s.sem, q_hi_s.at(b, n + 1))
                    dve.scalar_tensor_tensor(out=q_lo[:, n, :], in0=bank[:, :], scalar=bq_col[:, n:n + 1],
                                             in1=q_hi[:, n, :], op0=ALU.add, op1=ALU.subtract)\
                       .then_inc(q_lo_s.sem, 1)
                if kind == "K":
                    dve.wait_ge(k_hi_s.sem, k_hi_s.at(b, n + 1))
                    dve.scalar_tensor_tensor(out=k_lo[:, n, :], in0=bank[:, :], scalar=bk_col[:, n:n + 1],
                                             in1=k_hi[:, n, :], op0=ALU.add, op1=ALU.subtract)\
                       .then_inc(k_lo_s.sem, 1)
                if kind == "V":
                    dve.wait_ge(v_ps.sem, v_ps.at(b, n + 1))
                    dve.scalar_tensor_tensor(out=v_buf[par][:, n, :], in0=bank[:, :], scalar=UNW,
                                             in1=bv_row[:, :], op0=ALU.mult, op1=ALU.add)\
                       .then_inc(v_ready.sem, 1)

            def step(i, par, tables, with_d, with_b):
                def add_probs(s):
                    g, kt = s // TT, s % TT
                    dve.wait_ge(exp_done.sem, exp_done.at(i, 2 * s + 2))
                    if kt == 2:
                        dve.wait_ge(sum_first.sem, sum_first.at(i, g + 1))
                    else:
                        dve.wait_ge(sum_more.sem, sum_more.at(i, 2 * g + 1))
                    dve.tensor_tensor(prob_sum[:, :, :], prob_sum[:, :, :], probs[s % RING], ALU.add)\
                       .then_inc(sum_more.sem, 1)

                def scale_o(g):
                    dve.wait_ge(den_ps.sem, den_ps.at(i, g + 1))
                    if g >= 1:
                        dve.wait_ge(o_scaled.sem, o_scaled.at(i, g))
                    dve.reciprocal(inv_den[:, :], den[:, :]).then_inc(inv_ready.sem, 1)
                    dve.wait_ge(inv_ready.sem, inv_ready.at(i, g + 1))
                    dve.wait_ge(o_copied.sem, o_copied.at(i, g + 1))
                    dve.tensor_tensor(o_buf[:, :], o_buf[:, :], inv_den[:, :], ALU.mult).then_inc(o_scaled.sem, 1)

                if with_b:
                    dve.wait_ge(x_in.sem, x_in.at(i + 1, DMA))
                    for t in range(TT):
                        dve.bn_stats(stats[:, t, :], x_buf[1 - par][:, t, :]).then_inc(stats1.sem, 1)
                    moments(range(TT), stats1, moments1, i + 1, 0)
                for s in range(STEPS):
                    if with_b:
                        for kind, n in A_AT[s]:
                            a_part(i + 1, 1 - par, kind, n)
                    if with_d and s % TT >= 2:
                        add_probs(s)
                    if with_d and s >= 5 and (s - 5) % TT == 0:
                        scale_o((s - 5) // TT)
                if with_d:
                    scale_o(GROUPS - 1)
                if with_b:
                    for kind, n in A_TAIL:
                        a_part(i + 1, 1 - par, kind, n)
                bank_of = tables[2]
                for kind, n in phase2(with_d, with_b):
                    bank = None if kind == "B" else work[bank_of[kind, n]]
                    if kind == "B":
                        dve.wait_ge(max_ps.sem, max_ps.at(i + 1, n + 1))
                        dve.tensor_reduce(maxima[:, 2 * n:2 * n + 2], scores[n % 2][:, :, :], AX_X, ALU.max)\
                           .then_inc(max_done.sem, 1)
                        if n % (MAX_UNITS // 2) == MAX_UNITS // 2 - 1:
                            half = n // (MAX_UNITS // 2)
                            c = slice(MAX_UNITS * half, MAX_UNITS * (half + 1))
                            dve.wait_ge(max_done.sem, max_done.at(i + 1, n + 1))
                            dve.tensor_scalar(neg_max[:, c], maxima[:, c], -1.0 / MAX_UNIT, None, ALU.mult)\
                               .then_inc(negmax_s.sem, 1)
                    if kind == "OP":
                        dve.wait_ge(op_ps.sem, op_ps.at(i, n + 1))
                        dve.wait_ge(xbo_ready.sem, xbo_ready.at(i, n + 1))
                        dve.scalar_tensor_tensor(out=x_buf[par][:, n, :], in0=bank[:, :], scalar=UNW,
                                                 in1=x_buf[par][:, n, :], op0=ALU.mult, op1=ALU.add)\
                           .then_inc(x1_ready.sem, 1)
                        dve.wait_ge(x1_ready.sem, x1_ready.at(i, n + 1))
                        dve.bn_stats(stats[:, n, :], x_buf[par][:, n, :]).then_inc(stats2.sem, 1)
                        moments(range(n, n + 1), stats2, moments2, i, MOMENTS * n)
                    if kind == "LG":
                        link = iter(range(1, GATE_A + 1))
                        ops = TT * [None]
                        dve.wait_ge(logit_ps.sem, logit_ps.at(i, 1))
                        dve.scalar_tensor_tensor(
                            out=logits[:, :, :],
                            in0=bank[:, 0:TT * EXPERTS].rearrange("p (t e) -> p t e", t=TT), scalar=UNW,
                            in1=bg_row[:, :].unsqueeze(1).to_broadcast([P, TT, EXPERTS]),
                            op0=ALU.mult, op1=ALU.add).then_inc(gate_a.sem, 1)
                        dve.wait_ge(gate_a.sem, gate_a.at(i, 1))
                        other = logits[:, :, :].unsqueeze(2).to_broadcast([P, TT, EXPERTS, EXPERTS])
                        own = logits[:, :, :].unsqueeze(3).to_broadcast([P, TT, EXPERTS, EXPERTS])
                        tri = lower_tri[:, :, :].unsqueeze(1).to_broadcast([P, TT, EXPERTS, EXPERTS])
                        dve.tensor_reduce(top1[:, :], logits[:, :, :], AX_X, ALU.max).then_inc(gate_a.sem, 1)
                        dve.tensor_tensor(cmp_gt, other, own, ALU.is_gt).then_inc(gate_a.sem, 1)
                        dve.tensor_tensor(cmp_eq, other, own, ALU.is_equal).then_inc(gate_a.sem, 1)
                        dve.wait_ge(gate_a.sem, gate_a.at(i, 4))
                        dve.tensor_tensor(cmp_eq, cmp_eq, tri, ALU.mult).then_inc(gate_a.sem, 1)
                        dve.wait_ge(gate_a.sem, gate_a.at(i, 5))
                        dve.tensor_tensor(cmp_gt, cmp_gt, cmp_eq, ALU.add).then_inc(gate_a.sem, 1)
                        dve.wait_ge(gate_a.sem, gate_a.at(i, 6))
                        dve.tensor_reduce(rank[:, :, :], cmp_gt, AX_X, ALU.add).then_inc(gate_a.sem, 1)
                        dve.tensor_tensor(gap[:, :, :], logits[:, :, :],
                                          top1[:, :].unsqueeze(2).to_broadcast([P, TT, EXPERTS]),
                                          ALU.subtract).then_inc(gate_a.sem, 1)
                    if (kind, n) == ("W1", 1):
                        dve.wait_ge(gate_a.sem, gate_a.at(i, GATE_A))
                        dve.wait_ge(gate_exp_s.sem, gate_exp_s.at(i, 1))
                        dve.scalar_tensor_tensor(out=gates[:, :, :], in0=rank[:, :, :], scalar=2.0,
                                                 in1=gate_exp[:, :, :], op0=ALU.is_lt, op1=ALU.mult)\
                           .then_inc(gate_b.sem, 1)
                        dve.wait_ge(gate_b.sem, gate_b.at(i, 1))
                        dve.tensor_reduce(gate_den[:, 0, :], gates[:, :, :], AX_X, ALU.add).then_inc(gate_b.sem, 1)
                        dve.wait_ge(gate_b.sem, gate_b.at(i, 2))
                        dve.reciprocal(gate_den[:, 1, :], gate_den[:, 0, :]).then_inc(gate_b.sem, 1)
                        dve.wait_ge(gate_b.sem, gate_b.at(i, 3))
                        dve.tensor_tensor(gates[:, :, :], gates[:, :, :],
                                          gate_den[:, 1, :].unsqueeze(2).to_broadcast([P, TT, EXPERTS]),
                                          ALU.mult).then_inc(gate_b.sem, 1)
                        dve.wait_ge(gate_b.sem, gate_b.at(i, 4))
                        dve.tensor_copy(gate_pair[:, :, 0:EXPERTS], gates[:, :, :]).then_inc(gate_b.sem, 1)
                        dve.wait_ge(gate_b.sem, gate_b.at(i, 5))
                        dve.tensor_tensor(gate_pair[:, :, EXPERTS:2 * EXPERTS], gates[:, :, :],
                                          gate_pair[:, :, 0:EXPERTS], ALU.subtract).then_inc(gate_b.sem, 1)
                    if kind == "GB":
                        dve.wait_ge(gbc_ps.sem, gbc_ps.at(i, n + 1))
                        dve.wait_ge(h_ready.sem, h_ready.at(i, n + 1))
                        if n >= 2:
                            dve.wait_ge(gh_lo_s.sem, gh_lo_s.at(i, n - 1))
                        dve.tensor_tensor(gh32[:, n % 2, :], bank[:, :], h_buf[:, n, :], ALU.mult)\
                           .then_inc(gh32_s.sem, 1)
                    if kind == "W2":
                        dve.wait_ge(w2_ps.sem, w2_ps.at(i, n + 1))
                        dve.scalar_tensor_tensor(out=x_buf[par][:, n, :], in0=bank[:, :], scalar=SCALING * UNW,
                                                 in1=x_buf[par][:, n, :], op0=ALU.mult, op1=ALU.add)\
                           .then_inc(out_ready.sem, 1)

            run_steps(dve, step)

        @block.tensor
        def _(pe):
            pe.wait_ge(ln_const.sem, 4)
            pe.wait_ge(setup_hi.sem, len(weights) + 3)
            pe.wait_ge(setup_lo.sem, len(weights) + 3)

            def three(dst, lhs_hi, lhs_lo, rhs_hi, rhs_lo, tiles):
                for t in range(tiles):
                    pe.matmul(dst, lhs_hi(t), rhs_hi(t), start=(t == 0), stop=False)
                    pe.matmul(dst, lhs_hi(t), rhs_lo(t), start=False, stop=False)
                    last = pe.matmul(dst, lhs_lo(t), rhs_hi(t), start=False, stop=(t == tiles - 1))
                return last

            def free(i, prior):
                if prior is None:
                    return
                kind, n, offset = prior
                sem = bank_read[kind]
                pe.wait_ge(sem.sem, sem.at(i + offset, n + 1))

            def a_part(i, kind, n, prior, par_next):
                b = i + 1
                free(i, prior[kind, n])
                bank = work[BANK_A[kind, n]]
                cols = slice(P * n, P * n + P)
                if kind == "CT":
                    if n == 0:
                        pe.wait_ge(ctx_in.sem, ctx_in.at(b, DMA))
                    for t in range(DT):
                        last = pe.transpose(bank[:, P * t:P * t + P], ctx_buf[:, n, P * t:P * t + P], ident32[:, :])
                    last.then_inc(ctxT_ps.sem, 1)
                if kind == "XT":
                    pe.wait_ge(xn_ready.sem, xn_ready.at(b, n + 1))
                    for t in range(DT):
                        last = pe.transpose(bank[:, P * t:P * t + P], xn[:, n % 2, P * t:P * t + P], ident32[:, :])
                    last.then_inc(xT_ps.sem, 1)
                if kind == "Q":
                    if n == 0:
                        pe.wait_ge(xT_lo_s.sem, xT_lo_s.at(b, TT))
                    three(bank[:, :], lambda t: w_hi["q"][:, t, cols], lambda t: w_lo["q"][:, t, cols],
                          lambda t: xT_hi[:, t, :], lambda t: xT_lo[:, t, :], DT).then_inc(q_ps.sem, 1)
                if kind == "K":
                    if n == 0:
                        pe.wait_ge(ctxT_lo_s.sem, ctxT_lo_s.at(b, TT))
                    three(bank[:, :], lambda t: w_hi["k"][:, t, cols], lambda t: w_lo["k"][:, t, cols],
                          lambda t: ctxT_hi[:, t, :], lambda t: ctxT_lo[:, t, :], DT).then_inc(k_ps.sem, 1)
                if kind == "V":
                    three(bank[:, :], lambda t: ctxT_hi[:, t, cols], lambda t: ctxT_lo[:, t, cols],
                          lambda t: w_hi["v"][:, t, :], lambda t: w_lo["v"][:, t, :], DT).then_inc(v_ps.sem, 1)

            def step(i, par, tables, with_d, with_b):
                prior_a, (oT_prior, den_prior), bank_of, prior_d, _ = tables

                def score_step(s):
                    g, kt = s // TT, s % TT
                    if s == 0:
                        pe.wait_ge(maxrow_in[0].sem, maxrow_in[0].at(i, DMA))
                    if s == STEPS // 2:
                        pe.wait_ge(maxrow_in[1].sem, maxrow_in[1].at(i, DMA))
                    for pr in range(2):
                        if s >= 1:
                            pe.wait_ge(exp_done.sem, exp_done.at(i, 2 * s - 1 + pr))
                        else:
                            pe.wait_ge(max_done.sem, max_done.at(i, MAX_UNITS - 1 + pr))
                        for j in range(2):
                            h = HT * g + 2 * pr + j
                            last = pe.matmul(scores[pr][:, j, :], k_stack[0:STACK + 1, h, P * kt:P * kt + P],
                                             q_stack[0:STACK + 1, h, :], start=True, stop=True)
                        last.then_inc(score_ps.sem, 1)

                def values_step(s):
                    g, kt = s // TT, s % TT
                    if s == 0:
                        free(i, oT_prior)
                        pe.wait_ge(v_ready.sem, v_ready.at(i, TT))
                    elif kt == 0:
                        pe.wait_ge(o_copied.sem, o_copied.at(i, g))
                    pe.wait_ge(exp_done.sem, exp_done.at(i, 2 * s + 2))
                    for j in range(HT):
                        h = HT * g + j
                        last = pe.matmul(oT[DK * j:DK * j + DK, :], v_buf[par][:, kt, DK * h:DK * h + DK],
                                         probs[s % RING][:, j, :], start=(kt == 0), stop=(kt == TT - 1))
                    last.then_inc(pv_done.sem, 1)

                def denominators(g):
                    if g == 0:
                        free(i, den_prior)
                    else:
                        pe.wait_ge(inv_ready.sem, inv_ready.at(i, g))
                    pe.wait_ge(sum_more.sem, sum_more.at(i, 2 * g + 2))
                    for j in range(HT):
                        last = pe.matmul(den[DK * j:DK * j + DK, :], ones[:, :], prob_sum[:, j, :],
                                         start=True, stop=True)
                    last.then_inc(den_ps.sem, 1)

                for s in range(STEPS):
                    if with_d:
                        score_step(s)
                    if with_b:
                        for kind, n in A_AT[s]:
                            a_part(i, kind, n, prior_a, None)
                    if with_d and s >= 1:
                        values_step(s - 1)
                    if with_d and s >= 5 and (s - 5) % TT == 0:
                        denominators((s - 5) // TT)
                if with_d:
                    values_step(STEPS - 1)
                    denominators(GROUPS - 1)
                if with_b:
                    for kind, n in A_TAIL:
                        a_part(i, kind, n, prior_a, None)

                for kind, n in phase2(with_d, with_b):
                    if kind == "B":
                        h, qt = n // 2, 2 * (n % 2)
                        if n == 0:
                            pe.wait_ge(stack_in[0].sem, stack_in[0].at(i + 1, 24 * DMA))
                            if with_d:
                                pe.wait_ge(exp_done.sem, exp_done.at(i, 2 * STEPS))
                        if n == MAX_UNITS // 2:
                            pe.wait_ge(stack_in[1].sem, stack_in[1].at(i + 1, 24 * DMA))
                        if n >= 2:
                            pe.wait_ge(max_done.sem, max_done.at(i + 1, n - 1))
                        for j in range(2):
                            q = P * (qt + j)
                            last = pe.matmul(scores[n % 2][:, j, :], q_stack[0:STACK, h, q:q + P],
                                             k_stack[0:STACK, h, :], start=True, stop=True)
                        last.then_inc(max_ps.sem, 1)
                        continue
                    free(i, prior_d[kind, n])
                    bank = work[bank_of[kind, n]]
                    cols = slice(P * n, P * n + P)
                    if kind == "MT":
                        pe.wait_ge(negmax_s.sem, negmax_s.at(i + 1, n + 1))
                        pe.transpose(bank[:, :].bitcast(F16)[0:MAX_UNITS, 0:P],
                                     neg_max[:, MAX_UNITS * n:MAX_UNITS * (n + 1)], ident16[:, :])\
                          .then_inc(maxT_ps.sem, 1)
                    if kind == "OP":
                        if n == 0:
                            pe.wait_ge(o_lo_s.sem, o_lo_s.at(i, GROUPS))
                        three(bank[:, :], lambda t: o_hi[:, t, cols], lambda t: o_lo[:, t, cols],
                              lambda t: w_hi["o"][:, t, :], lambda t: w_lo["o"][:, t, :], DT).then_inc(op_ps.sem, 1)
                    if kind == "T":
                        pe.wait_ge(x1n_ready.sem, x1n_ready.at(i, n + 1))
                        for t in range(DT):
                            last = pe.transpose(bank[:, P * t:P * t + P], xn[:, n % 2, P * t:P * t + P], ident32[:, :])
                        last.then_inc(x1T_ps.sem, 1)
                    if kind == "LG":
                        pe.wait_ge(x1T_lo_s.sem, x1T_lo_s.at(i, TT))
                        for m in range(TT):
                            tok = slice(P * m, P * m + P)
                            last = three(bank[:, EXPERTS * m:EXPERTS * (m + 1)],
                                         lambda t: xT_hi[:, t, tok], lambda t: xT_lo[:, t, tok],
                                         lambda t: wg_hi[:, t, :], lambda t: wg_lo[:, t, :], DT)
                        last.then_inc(logit_ps.sem, 1)
                    if kind == "W1":
                        three(bank[:, :], lambda t: w_hi["1"][:, t, cols], lambda t: w_lo["1"][:, t, cols],
                              lambda t: xT_hi[:, t, :], lambda t: xT_lo[:, t, :], DT).then_inc(w1_ps.sem, 1)
                    if kind == "GT":
                        pe.wait_ge(gate_b.sem, gate_b.at(i, GATE_B))
                        for m in range(TT):
                            last = pe.transpose(bank[:, :].bitcast(F16)[0:2 * EXPERTS, P * m:P * m + P],
                                                gate_pair[:, m, :], ident16[:, :])
                        last.then_inc(gateT_ps.sem, 1)
                    if kind == "GB":
                        if n == 0:
                            pe.wait_ge(gateT_s.sem, gateT_s.at(i, 1))
                        pe.matmul(bank[:, :], select16[:, n, :], gateT[:, :], start=True, stop=True)\
                          .then_inc(gbc_ps.sem, 1)
                    if kind == "W2":
                        if n == 0:
                            pe.wait_ge(gh_lo_s.sem, gh_lo_s.at(i, DT))
                        three(bank[:, :], lambda t: gh_hi[:, t, cols], lambda t: gh_lo[:, t, cols],
                              lambda t: w_hi["2"][:, t, :], lambda t: w_lo["2"][:, t, :], DT).then_inc(w2_ps.sem, 1)

            run_steps(pe, step)


def kernel(**inputs):
    import concourse.bacc as _bacc
    from concourse.bass_utils import run_bass_kernel_spmd as _run

    def flip(name):
        a = np.asarray(inputs[name])
        return np.ascontiguousarray(a.reshape(-1, a.shape[-1]).T)

    def by_partition(name):
        return np.ascontiguousarray(np.asarray(inputs[name]).reshape(-1, P).T)

    w2 = np.asarray(inputs["L0_ffn_W2"])
    experts = w2.shape[0]
    er = experts * w2.shape[2]
    select = np.zeros((2 * experts, er), np.float32)
    for e in range(experts):
        select[[e, experts + e], e * (er // experts):(e + 1) * (er // experts)] = 1.0
    arrays = {
        "x": inputs["x"], "ctx": inputs["ctx_1024"],
        "wq_t": flip("L0_xattn_Wq"), "bq": by_partition("L0_xattn_bq"),
        "wk_t": flip("L0_xattn_Wk"), "bk": by_partition("L0_xattn_bk"),
        "wv_t": flip("L0_xattn_Wv"), "bv": inputs["L0_xattn_bv"],
        "wo_t": flip("L0_xattn_Wo"), "bo": inputs["L0_xattn_bo"],
        "wg_t": flip("L0_ffn_Wg"), "bg": inputs["L0_ffn_bg"],
        "w1_t": flip("L0_ffn_W1"),
        "w2_t": np.ascontiguousarray(w2.transpose(0, 2, 1).reshape(er, w2.shape[1])),
        "ident": np.eye(P, dtype=np.float32), "select": select,
        "lower": np.tril(np.ones((experts, experts), np.float32), -1),
    }
    arrays = {n: np.ascontiguousarray(a) for n, a in arrays.items()}
    nc = _bacc.Bacc("TRN2", target_bir_lowering=False, num_devices=1, dynamic_dma_scratch_size=4096)
    args = [nc.dram_tensor(n, a.shape, mybir.dt.from_np(a.dtype), kind="ExternalInput").ap()
            for n, a in arrays.items()]
    out = nc.dram_tensor("out", arrays["x"].shape, F32, kind="ExternalOutput").ap()
    xattn_moe_kernel(nc, *args, out)
    r = _run(nc, [arrays], core_ids=[0])
    return r.results[0]["out"]
```

```python
from contextlib import ExitStack

import concourse.bass as bass
from concourse import mybir
import numpy as np

F32 = mybir.dt.float32
F16 = mybir.dt.float16
ALU = mybir.AluOpType
ACT = mybir.ActivationFunctionType
AX_X = mybir.AxisListType.X

P = 128
HEADS = 16
DK = 32
EXPERTS = 8
LN_EPS = 1e-5
SCALE_W = 64.0
MAX_UNIT = SCALE_W * SCALE_W
SCALING = 2.0
DMA = 16


class Count:

    def __init__(self, sem, per):
        self.sem, self.per = sem, per

    def at(self, b, n):
        return b * self.per + n


def xattn_moe_kernel(nc, x, ctx, wq_t, bq, wk_t, bk, wv_t, bv, wo_t, bo, wg_t, bg, w1_t, w2_t,
                     ident, select, lower, out):
    B, T, D = x.shape
    TT = T // P
    DT = D // P
    HT = P // DK
    GROUPS = HEADS // HT
    EXP_SCALE = 1.0 / (MAX_UNIT * float(np.sqrt(np.float32(DK))))
    UNW = 1.0 / SCALE_W
    STACK = 3 * DK
    MAX_UNITS = HEADS * TT // 2
    RING = 3
    LN_STEPS = 8

    with ExitStack() as st:
        def sb(name, shape, dt):
            return st.enter_context(nc.sbuf_tensor(name, shape, dt))

        def pb(name, shape, dt):
            return st.enter_context(nc.psum_tensor(name, shape, dt))

        def count(name, per):
            return Count(st.enter_context(nc.semaphore(name)), per)

        w_hi = {n: sb(f"w{n}_hi", [P, DT, D], F16) for n in ("q", "k", "v", "o", "1", "2")}
        w_lo = {n: sb(f"w{n}_lo", [P, DT, D], F16) for n in ("q", "k", "v", "o", "1", "2")}
        wg_hi = sb("wg_hi", [P, DT, EXPERTS], F16)
        wg_lo = sb("wg_lo", [P, DT, EXPERTS], F16)
        bq_col = sb("bq_col", [P, DT], F32)
        bk_col = sb("bk_col", [P, DT], F32)
        bv_col = sb("bv_col", [P, DT], F32)
        bv_hi = sb("bv_hi", [P, DT], F16)
        bv_lo = sb("bv_lo", [P, DT], F16)
        bo_row = sb("bo_row", [P, D], F32)
        bg_row = sb("bg_row", [P, EXPERTS], F32)
        ident32 = sb("ident32", [P, P], F32)
        ident16 = sb("ident16", [P, P], F16)
        select16 = sb("select16", [2 * EXPERTS, DT, P], F16)
        lower_tri = sb("lower_tri", [P, EXPERTS, EXPERTS], F32)
        ones = sb("ones", [P, DK], F32)
        minus_half = sb("minus_half", [P, TT], F32)
        three_halves = sb("three_halves", [P, TT], F32)

        x_buf = [sb(f"x_buf{p}", [P, TT, D], F32) for p in range(2)]
        ctx_buf = sb("ctx_buf", [P, TT, D], F32)
        xn = sb("xn", [P, TT, D], F32)
        ctxT_hi = sb("ctxT_hi", [P, DT, T], F16)
        ctxT_lo = sb("ctxT_lo", [P, DT, T], F16)
        xT_hi = sb("xT_hi", [P, DT, T], F16)
        xT_lo = sb("xT_lo", [P, DT, T], F16)
        q_hi = sb("q_hi", [P, DT, T], F16)
        q_lo = sb("q_lo", [P, DT, T], F16)
        k_hi = sb("k_hi", [P, DT, T], F16)
        k_lo = sb("k_lo", [P, DT, T], F16)
        q_stack = sb("q_stack", [P, HEADS, T], F16)
        k_stack = sb("k_stack", [P, HEADS, T], F16)
        v_buf = [sb(f"v_buf{p}", [P, TT, D], F32) for p in range(2)]
        shared = sb("shared", [P, (RING + 1) * HT * T], F32)
        probs = [shared[:, s * HT * T:(s + 1) * HT * T].rearrange("p (j q) -> p j q", j=HT)
                 for s in range(RING)]
        prob_sum = shared[:, RING * HT * T:(RING + 1) * HT * T].rearrange("p (j q) -> p j q", j=HT)
        h_buf = probs[0]
        gh_hi = shared[:, HT * T:HT * T + HT * T // 2].bitcast(F16).rearrange("p (j q) -> p j q", j=HT)
        gh_lo = shared[:, HT * T + HT * T // 2:2 * HT * T].bitcast(F16).rearrange("p (j q) -> p j q", j=HT)
        gh32 = probs[2][:, 0:2, :]
        x1T32 = probs[2][:, 2:4, :]
        cmp_gt = prob_sum[:, 0, 0:TT * EXPERTS * EXPERTS].rearrange("p (t e j) -> p t e j", t=TT, e=EXPERTS)
        cmp_eq = prob_sum[:, 1, 0:TT * EXPERTS * EXPERTS].rearrange("p (t e j) -> p t e j", t=TT, e=EXPERTS)
        stage = [shared[:, n * DT * D:(n + 1) * DT * D].rearrange("p (t d) -> p t d", t=DT) for n in range(2)]

        o_buf = sb("o_buf", [P, T], F32)
        inv_den = sb("inv_den", [P, T], F32)
        o_hi = sb("o_hi", [P, DT, T], F16)
        o_lo = sb("o_lo", [P, DT, T], F16)
        maxima = sb("maxima", [P, HEADS * TT], F32)
        neg_max = sb("neg_max", [P, HEADS * TT], F16)
        max_rows = sb("max_rows", [HEADS * TT // 2, 2, P], F16)
        stats = sb("stats", [P, TT, 6], F32)
        moment_tmp = sb("moment_tmp", [P, 4, TT], F32)
        ln_tmp = sb("ln_tmp", [P, 8, TT], F32)
        logits = sb("logits", [P, TT, EXPERTS], F32)
        top1 = sb("top1", [P, TT], F32)
        rank = sb("rank", [P, TT, EXPERTS], F32)
        gap = sb("gap", [P, TT, EXPERTS], F32)
        gate_exp = sb("gate_exp", [P, TT, EXPERTS], F32)
        gate_den = sb("gate_den", [P, 2, TT], F32)
        gates = sb("gates", [P, TT, EXPERTS], F32)
        gate_pair = sb("gate_pair", [P, TT, 2 * EXPERTS], F16)
        gateT = sb("gateT", [2 * EXPERTS, T], F16)

        scores = [pb(f"scores{n}", [P, 2, T], F32) for n in range(2)]
        work = [pb(f"work{n}", [P, T], F32) for n in range(4)]
        oT, den = work[2], work[3]

        const_in = count("const_in", 0)
        stage_in = [count(f"stage_in{n}", 0) for n in range(2)]
        ln_const = count("ln_const", 0)
        setup_hi = count("setup_hi", 0)
        setup_lo = count("setup_lo", 0)
        SETUP_HI, SETUP_LO = 10, 10
        bo_ps = count("bo_ps", 0)
        bo_ready = count("bo_ready", 0)
        x_in = count("x_in", DMA)
        ctx_in = count("ctx_in", DMA)
        stack_in = [count(f"stack_in{n}", 24 * DMA) for n in range(2)]
        maxrow_in = [count(f"maxrow_in{n}", DMA) for n in range(2)]
        out_stored = count("out_stored", TT * DMA)
        stats1 = count("stats1", TT)
        MOMENTS = 6
        moments1 = count("moments1", MOMENTS)
        ln1_step = count("ln1_step", LN_STEPS)
        xn_ready = count("xn_ready", TT)
        xbo_ready = count("xbo_ready", TT)
        ctxT_ps = count("ctxT_ps", TT)
        ctxT_hi_s = count("ctxT_hi_s", TT)
        ctxT_lo_s = count("ctxT_lo_s", TT)
        xT_ps = count("xT_ps", TT)
        xT_hi_s = count("xT_hi_s", TT)
        xT_lo_s = count("xT_lo_s", TT)
        q_ps = count("q_ps", DT)
        q_hi_s = count("q_hi_s", DT)
        q_lo_s = count("q_lo_s", DT)
        k_ps = count("k_ps", DT)
        k_hi_s = count("k_hi_s", DT)
        k_lo_s = count("k_lo_s", DT)
        v_ps = count("v_ps", TT)
        v_ready = count("v_ready", TT)
        max_ps = count("max_ps", MAX_UNITS)
        max_done = count("max_done", MAX_UNITS)
        negmax_s = count("negmax_s", 2)
        maxT_ps = count("maxT_ps", 2)
        maxrow_s = count("maxrow_s", 2)
        STEPS = GROUPS * TT
        score_ps = count("score_ps", 2 * STEPS)
        exp_done = count("exp_done", 2 * STEPS)
        pv_done = count("pv_done", STEPS)
        sum_pool = count("sum_pool", 2 * GROUPS)
        sum_dve = count("sum_dve", GROUPS)
        den_ps = count("den_ps", GROUPS)
        o_copied = count("o_copied", GROUPS)
        inv_ready = count("inv_ready", GROUPS)
        o_scaled = count("o_scaled", GROUPS)
        o_hi_s = count("o_hi_s", GROUPS)
        o_lo_s = count("o_lo_s", GROUPS)
        op_ps = count("op_ps", TT)
        x1_ready = count("x1_ready", TT)
        stats2 = count("stats2", TT)
        moments2 = count("moments2", MOMENTS * TT)
        ln2_step = count("ln2_step", LN_STEPS * TT)
        x1n_ready = count("x1n_ready", TT)
        x1T_ps = count("x1T_ps", TT)
        x1T_hi_s = count("x1T_hi_s", TT)
        x1T_copied = count("x1T_copied", TT)
        x1T_lo_s = count("x1T_lo_s", TT)
        logit_ps = count("logit_ps", 1)
        GATE_A, GATE_B = 8, 6
        gate_a = count("gate_a", GATE_A)
        gate_exp_s = count("gate_exp_s", 1)
        gate_b = count("gate_b", GATE_B)
        gateT_ps = count("gateT_ps", 1)
        gateT_s = count("gateT_s", 1)
        w1_ps = count("w1_ps", DT)
        h_ready = count("h_ready", DT)
        gbc_ps = count("gbc_ps", DT)
        gh32_s = count("gh32_s", DT)
        gh_hi_s = count("gh_hi_s", DT)
        gh_lo_s = count("gh_lo_s", DT)
        w2_ps = count("w2_ps", TT)
        out_ready = count("out_ready", TT)

        bank_read = {"CT": ctxT_lo_s, "XT": xT_lo_s, "Q": q_lo_s, "K": k_lo_s, "V": v_ready,
                     "MT": maxrow_s, "OP": x1_ready, "T": x1T_copied, "LG": gate_a, "W1": h_ready,
                     "GT": gateT_s, "GB": gh32_s, "W2": out_ready, "O": o_copied, "DEN": inv_ready}

        A_AT = [[(u[:-1], int(u[-1])) for u in step.split()] for step in (
            "CT0 CT1", "CT2 CT3", "K0", "K1", "K2", "XT0 XT1", "XT2 XT3", "K3", "Q0", "Q1", "Q2", "Q3",
            "", "V0", "", "V1")]
        A_ORDER = [u for step in A_AT for u in step]
        STATS_AT = 3
        PHASE2 = ("B B B DEN3 OP0 B OP1 B V2 B B PO0 B PO1 B B OP2 PO2 B B OP3 PO3 B T0 B T1 B T2 B T3 V3 B B LG0 "
                  "W1_0 B B W1_1 MT0 GT0 GB0 W1_2 B B GB1 W1_3 GB2 B B GB3 B B B B W2_0 B B W2_1 B B W2_2 MT1 W2_3").split()

        def phase2(with_d, with_b):
            steps, units = [], 0
            for s in PHASE2:
                kind, n = (s.split("_") if "_" in s else (s.rstrip("0123456789"), s[-1]))
                if kind == "B":
                    if with_b:
                        steps.append(("B", units))
                    units += 1
                elif with_b if kind in ("MT", "V") else with_d:
                    steps.append((kind, int(n)))
            assert units == MAX_UNITS, units
            return steps

        def banks(uses, count_of_banks):
            return {u: n % count_of_banks for n, u in enumerate(uses)}

        def d_uses(with_d, with_b):
            return [u for u in phase2(with_d, with_b) if u[0] not in ("B", "DEN", "PO")]

        BANK_A = banks(A_ORDER, 2)

        def prior_uses(uses, bank_of, before):
            last, prior = dict(before), {}
            for kind, n, offset in uses:
                prior[kind, n] = last.get(bank_of[kind, n])
                last[bank_of[kind, n]] = (kind, n, offset)
            return prior, last

        def bank_tables(with_d, with_b, before):
            first, last = {}, dict(before)
            if with_b:
                first, last = prior_uses([(k, n, 1) for k, n in A_ORDER], BANK_A, last)
            if with_d:
                oT_prior, den_prior = last.get(2), last.get(3)
                last[2], last[3] = ("O", GROUPS - 1, 0), ("DEN", GROUPS - 1, 0)
            else:
                oT_prior = den_prior = None
            uses = d_uses(with_d, with_b)
            bank_of = banks(uses, 4)
            bank_of |= {("PO", n): bank for (k, n), bank in bank_of.items() if k == "OP"}
            second, last = prior_uses([(k, n, 1 if k in ("MT", "V") else 0) for k, n in uses], bank_of, last)
            return first, (oT_prior, den_prior), bank_of, second, last

        def shifted(last):
            return {bank: (k, n, offset - 1) for bank, (k, n, offset) in last.items()}

        PROLOGUE = bank_tables(False, True, {})
        FIRST = bank_tables(True, True, shifted(PROLOGUE[4]))
        MIDDLE = bank_tables(True, True, shifted(FIRST[4]))
        assert shifted(MIDDLE[4]) == shifted(FIRST[4])
        LAST = bank_tables(True, False, shifted(MIDDLE[4]))

        def run_steps(engine, step):
            step(-1, 1, PROLOGUE, False, True)
            step(0, 0, FIRST, True, True)
            with engine.Fori(1, B - 3, 2) as i:
                step(i, 1, MIDDLE, True, True)
                step(i + 1, 0, MIDDLE, True, True)
            step(B - 3, 1, MIDDLE, True, True)
            step(B - 2, 0, MIDDLE, True, True)
            step(B - 1, 1, LAST, True, False)

        x_tiles = x.rearrange("b (t p) d -> b p t d", p=P)
        ctx_tiles = ctx.rearrange("b (t p) d -> b p t d", p=P)
        out_tiles = out.rearrange("b (t p) d -> b t p d", p=P)
        weights = [("q", wq_t), ("k", wk_t), ("v", wv_t), ("o", wo_t), ("1", w1_t), ("2", w2_t)]

        block = st.enter_context(nc.Block())

        @block.sync
        def _(sp):
            def stack(b, half, hi, lo, hi_s, lo_s, dst, order):
                sp.wait_ge(hi_s.sem, hi_s.at(b, 2 * half + 2))
                sp.wait_ge(lo_s.sem, lo_s.at(b, 2 * half + 2))
                for g, part in enumerate(order):
                    src = hi if part == "hi" else lo
                    for j in range(HT):
                        heads = dst[DK * g:DK * g + DK, :, :].rearrange("p (t j) q -> p t j q", j=HT)
                        sp.dma_start(heads[:, 2 * half:2 * half + 2, j, :],
                                     src[DK * j:DK * j + DK, 2 * half:2 * half + 2, :])\
                          .then_inc(stack_in[half].sem, DMA)

            def step(i, par, tables, with_d, with_b):
                if with_d and with_b:
                    if not (isinstance(i, int) and i == 0):
                        sp.wait_ge(out_stored.sem, out_stored.at(i - 1, TT * DMA))
                    sp.dma_start(x_buf[1 - par][:, :, :], x_tiles[i + 1]).then_inc(x_in.sem, DMA)
                if with_b:
                    for half in range(2):
                        if with_d:
                            sp.wait_ge(score_ps.sem, score_ps.at(i, STEPS * (half + 1)))
                        stack(i + 1, half, k_hi, k_lo, k_hi_s, k_lo_s, k_stack, ("hi", "lo", "hi"))
                        stack(i + 1, half, q_hi, q_lo, q_hi_s, q_lo_s, q_stack, ("hi", "hi", "lo"))
                        if half == 0 and not (isinstance(i, int) and i + 2 >= B):
                            sp.wait_ge(ctxT_ps.sem, ctxT_ps.at(i + 1, TT))
                            sp.dma_start(ctx_buf[:, :, :], ctx_tiles[i + 2]).then_inc(ctx_in.sem, DMA)
                for kind, n in phase2(with_d, with_b):
                    if kind == "MT":
                        sp.wait_ge(maxrow_s.sem, maxrow_s.at(i + 1, n + 1))
                        half_heads = HEADS // 2
                        sp.dma_start(
                            q_stack[STACK:STACK + 1, half_heads * n:half_heads * (n + 1), :],
                            max_rows[:, n, :]).then_inc(maxrow_in[n].sem, DMA)
                    if kind == "W2":
                        sp.wait_ge(out_ready.sem, out_ready.at(i, n + 1))
                        sp.dma_start(out_tiles[i, n], x_buf[par][:, n, :]).then_inc(out_stored.sem, DMA)

            sp.dma_start(ctx_buf[:, :, :], ctx_tiles[0]).then_inc(ctx_in.sem, DMA)
            sp.dma_start(x_buf[0][:, :, :], x_tiles[0]).then_inc(x_in.sem, DMA)
            sp.dma_start(ident32[:, :], ident).then_inc(const_in.sem, DMA)
            sp.dma_start(bq_col[:, :], bq).then_inc(const_in.sem, DMA)
            sp.dma_start(bk_col[:, :], bk).then_inc(const_in.sem, DMA)
            sp.dma_start(bv_col[:, :], bv).then_inc(const_in.sem, DMA)
            sp.dma_start(bo_row[:, :], bo.partition_broadcast(P)).then_inc(const_in.sem, DMA)
            sp.dma_start(bg_row[:, :], bg.partition_broadcast(P)).then_inc(const_in.sem, DMA)
            sp.dma_start(lower_tri[:, :, :], lower.partition_broadcast(P)).then_inc(const_in.sem, DMA)
            sp.dma_start(o_buf[:, 0:DT * EXPERTS].rearrange("p (t e) -> p t e", t=DT),
                         wg_t.rearrange("(t p) e -> p t e", p=P))\
              .then_inc(const_in.sem, DMA)
            sp.dma_start(inv_den[0:2 * EXPERTS, :], select).then_inc(const_in.sem, DMA)
            for n, (_, w) in enumerate(weights):
                if n >= 2:
                    sp.wait_ge(setup_lo.sem, n - 1)
                sp.dma_start(stage[n % 2], w.rearrange("(t p) d -> p t d", p=P)).then_inc(stage_in[n % 2].sem, DMA)
            run_steps(sp, step)
            sp.wait_ge(out_stored.sem, out_stored.at(B, 0))

        @block.gpsimd
        def _(pool):
            pool.memset(minus_half[:, :], -0.5).then_inc(ln_const.sem, 1)
            pool.memset(three_halves[:, :], 1.5).then_inc(ln_const.sem, 1)

            def inv_std(b, tiles, base, step_s):
                c = slice(tiles[0], tiles[-1] + 1)
                mean2, var, first, sq, half, factor, inv, neg = (ln_tmp[:, n, c] for n in range(8))
                mh, th = minus_half[:, c], three_halves[:, c]
                for n, (dst, lhs, rhs, op) in enumerate([
                        (first, var, mh, ALU.pow), (sq, first, first, ALU.mult), (half, sq, var, ALU.mult),
                        (half, half, mh, ALU.mult), (factor, half, th, ALU.add), (inv, first, factor, ALU.mult),
                        (neg, mean2, inv, ALU.mult), (neg, neg, mh, ALU.mult)]):
                    if n:
                        pool.wait_ge(step_s.sem, step_s.at(b, base + n))
                    pool.tensor_tensor(dst, lhs, rhs, op).then_inc(step_s.sem, 1)

            def add_bo(b, par):
                pool.wait_ge(xn_ready.sem, xn_ready.at(b, TT))
                for t in range(TT):
                    pool.tensor_tensor(x_buf[par][:, t, :], x_buf[par][:, t, :], bo_row[:, :], ALU.add)\
                        .then_inc(xbo_ready.sem, 1)

            def step(i, par, tables, with_d, with_b):
                for s in range(STEPS):
                    if with_d and s % TT in (1, 2):
                        g = s // TT
                        pool.wait_ge(exp_done.sem, exp_done.at(i, 2 * s + 2))
                        if s % TT == 1 and g >= 1:
                            pool.wait_ge(den_ps.sem, den_ps.at(i, g))
                        if s % TT == 2:
                            pool.wait_ge(sum_pool.sem, sum_pool.at(i, 2 * g + 1))
                        pool.tensor_tensor(prob_sum[:, :, :], probs[(s - 1) % RING] if s % TT == 1 else prob_sum,
                                           probs[s % RING], ALU.add).then_inc(sum_pool.sem, 1)
                    if with_b and s == STATS_AT:
                        pool.wait_ge(moments1.sem, moments1.at(i + 1, MOMENTS))
                        inv_std(i + 1, range(TT), 0, ln1_step)
                    if with_d and s >= 6 and (s - 6) % TT == 0:
                        o_low(i, (s - 6) // TT)
                    if with_b and s == 7:
                        add_bo(i + 1, 1 - par)
                for kind, n in phase2(with_d, with_b):
                    if kind == "DEN":
                        o_low(i, n)
                    if kind == "PO":
                        pool.wait_ge(moments2.sem, moments2.at(i, MOMENTS * (n + 1)))
                        inv_std(i, range(n, n + 1), LN_STEPS * n, ln2_step)
                    if kind == "T":
                        pool.wait_ge(x1T_hi_s.sem, x1T_hi_s.at(i, n + 1))
                        pool.wait_ge(x1T_copied.sem, x1T_copied.at(i, n + 1))
                        cols = slice(P * n, P * n + P)
                        pool.tensor_tensor(xT_lo[:, :, cols],
                                           x1T32[:, n % 2, :].rearrange("p (t c) -> p t c", t=DT),
                                           xT_hi[:, :, cols], ALU.subtract).then_inc(x1T_lo_s.sem, 1)
                    if kind == "GB":
                        pool.wait_ge(gh_hi_s.sem, gh_hi_s.at(i, n + 1))
                        pool.tensor_tensor(gh_lo[:, n, :], gh32[:, n % 2, :], gh_hi[:, n, :], ALU.subtract)\
                            .then_inc(gh_lo_s.sem, 1)

            def o_low(i, g):
                pool.wait_ge(o_hi_s.sem, o_hi_s.at(i, g + 1))
                pool.tensor_tensor(o_lo[:, g, :], o_buf[:, :], o_hi[:, g, :], ALU.subtract)\
                    .then_inc(o_lo_s.sem, 1)

            pool.wait_ge(ln_const.sem, 4)
            pool.wait_ge(bo_ready.sem, 1)
            run_steps(pool, step)

        @block.scalar
        def _(act):
            for n, (name, _) in enumerate(weights):
                act.wait_ge(stage_in[n % 2].sem, DMA * (n // 2 + 1))
                act.activation(w_hi[name][:, :, :], stage[n % 2], ACT.Copy, scale=SCALE_W).then_inc(setup_hi.sem, 1)
            act.wait_ge(const_in.sem, 9 * DMA)
            act.activation(wg_hi[:, :, :], o_buf[:, 0:DT * EXPERTS].rearrange("p (t e) -> p t e", t=DT),
                           ACT.Copy, scale=SCALE_W).then_inc(setup_hi.sem, 1)
            act.activation(ident16[:, :], ident32[:, :], ACT.Copy).then_inc(setup_hi.sem, 1)
            act.activation(select16[:, :, :], inv_den[0:2 * EXPERTS, :].rearrange("p (t c) -> p t c", t=DT),
                           ACT.Copy).then_inc(setup_hi.sem, 1)
            act.activation(bv_hi[:, :], bv_col[:, :], ACT.Copy).then_inc(setup_hi.sem, 1)
            act.wait_ge(setup_lo.sem, SETUP_LO)

            def copy_v(b, par, n, bank):
                act.wait_ge(v_ps.sem, v_ps.at(b, n + 1))
                act.activation(v_buf[par][:, n, :], bank[:, :], ACT.Copy, scale=UNW).then_inc(v_ready.sem, 1)

            def a_part(b, par, kind, n):
                cols = slice(P * n, P * n + P)
                bank = work[BANK_A[kind, n]]
                if kind == "CT":
                    act.wait_ge(ctxT_ps.sem, ctxT_ps.at(b, n + 1))
                    act.activation(ctxT_hi[:, :, cols], bank[:, :].rearrange("p (t c) -> p t c", t=DT), ACT.Copy)\
                       .then_inc(ctxT_hi_s.sem, 1)
                if kind == "XT":
                    act.wait_ge(xT_ps.sem, xT_ps.at(b, n + 1))
                    act.activation(xT_hi[:, :, cols], bank[:, :].rearrange("p (t c) -> p t c", t=DT), ACT.Copy)\
                       .then_inc(xT_hi_s.sem, 1)
                if kind == "Q":
                    act.wait_ge(q_ps.sem, q_ps.at(b, n + 1))
                    act.activation(q_hi[:, n, :], bank[:, :], ACT.Identity, bias=bq_col[:, n:n + 1])\
                       .then_inc(q_hi_s.sem, 1)
                if kind == "V":
                    copy_v(b, par, n, bank)
                if kind == "K":
                    act.wait_ge(k_ps.sem, k_ps.at(b, n + 1))
                    act.activation(k_hi[:, n, :], bank[:, :], ACT.Identity, bias=bk_col[:, n:n + 1])\
                       .then_inc(k_hi_s.sem, 1)

            def normalise(b, buf, t, step_s, steps, ready):
                act.wait_ge(step_s.sem, step_s.at(b, steps))
                act.activation(xn[:, t, :], buf[:, t, :], ACT.Identity, bias=ln_tmp[:, 7, t:t + 1],
                               scale=ln_tmp[:, 6, t:t + 1]).then_inc(ready.sem, 1)

            def step(i, par, tables, with_d, with_b):
                def copy_o(g):
                    act.wait_ge(pv_done.sem, pv_done.at(i, TT * (g + 1)))
                    if g >= 1:
                        act.wait_ge(o_lo_s.sem, o_lo_s.at(i, g))
                    act.activation(o_buf[:, :], oT[:, :], ACT.Copy).then_inc(o_copied.sem, 1)

                def o_high(g):
                    act.wait_ge(o_scaled.sem, o_scaled.at(i, g + 1))
                    act.activation(o_hi[:, g, :], o_buf[:, :], ACT.Copy).then_inc(o_hi_s.sem, 1)

                for s in range(STEPS):
                    if with_d:
                        for pr in range(2):
                            act.wait_ge(score_ps.sem, score_ps.at(i, 2 * s + pr + 1))
                            if s >= RING and pr == 0:
                                act.wait_ge(pv_done.sem, pv_done.at(i, s - RING + 1))
                                late = s - RING
                                if late % TT == 3:
                                    act.wait_ge(sum_dve.sem, sum_dve.at(i, late // TT + 1))
                                else:
                                    act.wait_ge(sum_pool.sem, sum_pool.at(i, 2 * (late // TT) + max(late % TT, 1)))
                            act.activation(probs[s % RING][:, 2 * pr:2 * pr + 2, :], scores[pr][:, :, :], ACT.Exp,
                                           scale=EXP_SCALE).then_inc(exp_done.sem, 1)
                    if with_b:
                        if s == STATS_AT + 1:
                            for t in range(TT):
                                normalise(i + 1, x_buf[1 - par], t, ln1_step, LN_STEPS, xn_ready)
                        for kind, n in A_AT[s]:
                            a_part(i + 1, 1 - par, kind, n)
                    if with_d and s % TT == 0 and s >= TT:
                        copy_o(s // TT - 1)
                    if with_d and s >= 6 and (s - 6) % TT == 0:
                        o_high((s - 6) // TT)
                bank_of = tables[2]
                for kind, n in phase2(with_d, with_b):
                    bank = None if kind in ("B", "DEN") else work[bank_of[kind, n]]
                    cols = slice(P * n, P * n + P)
                    if kind == "DEN":
                        copy_o(n)
                        o_high(n)
                    if kind == "V":
                        copy_v(i + 1, 1 - par, n, bank)
                    if kind == "PO":
                        normalise(i, x_buf[par], n, ln2_step, LN_STEPS * (n + 1), x1n_ready)
                    if kind == "T":
                        act.wait_ge(x1T_ps.sem, x1T_ps.at(i, n + 1))
                        act.activation(xT_hi[:, :, cols], bank[:, :].rearrange("p (t c) -> p t c", t=DT), ACT.Copy)\
                           .then_inc(x1T_hi_s.sem, 1)
                        if n >= 2:
                            act.wait_ge(x1T_lo_s.sem, x1T_lo_s.at(i, n - 1))
                        act.activation(x1T32[:, n % 2, :], bank[:, :], ACT.Copy).then_inc(x1T_copied.sem, 1)
                    if kind == "MT":
                        act.wait_ge(maxT_ps.sem, maxT_ps.at(i + 1, n + 1))
                        act.activation(max_rows[:, n, :], bank[:, :].bitcast(F16)[0:HEADS * TT // 2, 0:P], ACT.Copy)\
                           .then_inc(maxrow_s.sem, 1)
                    if kind == "LG":
                        act.wait_ge(gate_a.sem, gate_a.at(i, GATE_A))
                        act.activation(gate_exp[:, :, :], gap[:, :, :], ACT.Exp).then_inc(gate_exp_s.sem, 1)
                    if kind == "W1":
                        act.wait_ge(w1_ps.sem, w1_ps.at(i, n + 1))
                        act.activation(h_buf[:, n, :], bank[:, :], ACT.Gelu, scale=UNW).then_inc(h_ready.sem, 1)
                    if kind == "GT":
                        act.wait_ge(gateT_ps.sem, gateT_ps.at(i, 1))
                        act.activation(gateT[:, :], bank[:, :].bitcast(F16)[0:2 * EXPERTS, 0:T], ACT.Copy)\
                           .then_inc(gateT_s.sem, 1)
                    if kind == "GB":
                        act.wait_ge(gh32_s.sem, gh32_s.at(i, n + 1))
                        act.activation(gh_hi[:, n, :], gh32[:, n % 2, :], ACT.Copy).then_inc(gh_hi_s.sem, 1)

            run_steps(act, step)

        @block.vector
        def _(dve):
            dve.memset(ones[:, :], 1.0).then_inc(ln_const.sem, 1)
            dve.memset(k_stack[STACK:STACK + 1, :, :], MAX_UNIT).then_inc(ln_const.sem, 1)
            for n, (name, _) in enumerate(weights):
                dve.wait_ge(setup_hi.sem, n + 1)
                dve.scalar_tensor_tensor(out=w_lo[name][:, :, :], in0=stage[n % 2], scalar=SCALE_W,
                                         in1=w_hi[name][:, :, :], op0=ALU.mult, op1=ALU.subtract)\
                   .then_inc(setup_lo.sem, 1)
            dve.wait_ge(setup_hi.sem, len(weights) + 1)
            dve.scalar_tensor_tensor(out=wg_lo[:, :, :],
                                     in0=o_buf[:, 0:DT * EXPERTS].rearrange("p (t e) -> p t e", t=DT),
                                     scalar=SCALE_W, in1=wg_hi[:, :, :], op0=ALU.mult, op1=ALU.subtract)\
               .then_inc(setup_lo.sem, 1)
            dve.tensor_scalar(bq_col[:, :], bq_col[:, :], SCALE_W, None, ALU.mult).then_inc(setup_lo.sem, 1)
            dve.tensor_scalar(bk_col[:, :], bk_col[:, :], SCALE_W, None, ALU.mult).then_inc(setup_lo.sem, 1)
            dve.wait_ge(setup_hi.sem, SETUP_HI)
            dve.tensor_tensor(bv_lo[:, :], bv_col[:, :], bv_hi[:, :], ALU.subtract).then_inc(setup_lo.sem, 1)
            dve.wait_ge(setup_lo.sem, SETUP_LO)
            dve.wait_ge(bo_ps.sem, 1)
            dve.scalar_tensor_tensor(out=bo_row[:, :], in0=work[0][:, :], scalar=UNW, in1=bo_row[:, :],
                                     op0=ALU.mult, op1=ALU.add).then_inc(bo_ready.sem, 1)

            def moments(tiles, stats_s, moment_s, b, base):
                c = slice(tiles[0], tiles[-1] + 1)
                mean_a, m2_a, mean_b, m2_b = (stats[:, c, n] for n in (1, 2, 4, 5))
                diff, m2, sq, quarter = (moment_tmp[:, n, c] for n in range(4))
                dve.wait_ge(stats_s.sem, stats_s.at(b, tiles[-1] + 1))
                dve.tensor_tensor(ln_tmp[:, 0, c], mean_a, mean_b, ALU.add).then_inc(moment_s.sem, 1)
                dve.tensor_tensor(diff, mean_a, mean_b, ALU.subtract).then_inc(moment_s.sem, 1)
                dve.tensor_tensor(m2, m2_a, m2_b, ALU.add).then_inc(moment_s.sem, 1)
                dve.wait_ge(moment_s.sem, moment_s.at(b, base + 2))
                dve.tensor_tensor(sq, diff, diff, ALU.mult).then_inc(moment_s.sem, 1)
                dve.wait_ge(moment_s.sem, moment_s.at(b, base + 4))
                dve.tensor_scalar(quarter, sq, 0.25, LN_EPS, ALU.mult, ALU.add).then_inc(moment_s.sem, 1)
                dve.wait_ge(moment_s.sem, moment_s.at(b, base + 5))
                dve.scalar_tensor_tensor(out=ln_tmp[:, 1, c], in0=m2, scalar=1.0 / D, in1=quarter,
                                         op0=ALU.mult, op1=ALU.add).then_inc(moment_s.sem, 1)

            def a_part(b, kind, n):
                cols = slice(P * n, P * n + P)
                bank = work[BANK_A[kind, n]]
                tiles = bank[:, :].rearrange("p (t c) -> p t c", t=DT)
                if kind == "CT":
                    dve.wait_ge(ctxT_hi_s.sem, ctxT_hi_s.at(b, n + 1))
                    dve.tensor_tensor(ctxT_lo[:, :, cols], tiles, ctxT_hi[:, :, cols], ALU.subtract)\
                       .then_inc(ctxT_lo_s.sem, 1)
                if kind == "XT":
                    dve.wait_ge(xT_hi_s.sem, xT_hi_s.at(b, n + 1))
                    dve.tensor_tensor(xT_lo[:, :, cols], tiles, xT_hi[:, :, cols], ALU.subtract)\
                       .then_inc(xT_lo_s.sem, 1)
                if kind == "Q":
                    dve.wait_ge(q_hi_s.sem, q_hi_s.at(b, n + 1))
                    dve.scalar_tensor_tensor(out=q_lo[:, n, :], in0=bank[:, :], scalar=bq_col[:, n:n + 1],
                                             in1=q_hi[:, n, :], op0=ALU.add, op1=ALU.subtract)\
                       .then_inc(q_lo_s.sem, 1)
                if kind == "K":
                    dve.wait_ge(k_hi_s.sem, k_hi_s.at(b, n + 1))
                    dve.scalar_tensor_tensor(out=k_lo[:, n, :], in0=bank[:, :], scalar=bk_col[:, n:n + 1],
                                             in1=k_hi[:, n, :], op0=ALU.add, op1=ALU.subtract)\
                       .then_inc(k_lo_s.sem, 1)

            def step(i, par, tables, with_d, with_b):
                def add_last_probs(s):
                    g = s // TT
                    dve.wait_ge(exp_done.sem, exp_done.at(i, 2 * s + 2))
                    dve.wait_ge(sum_pool.sem, sum_pool.at(i, 2 * g + 2))
                    dve.tensor_tensor(prob_sum[:, :, :], prob_sum[:, :, :], probs[s % RING], ALU.add)\
                       .then_inc(sum_dve.sem, 1)

                def scale_o(g):
                    dve.wait_ge(den_ps.sem, den_ps.at(i, g + 1))
                    if g >= 1:
                        dve.wait_ge(o_scaled.sem, o_scaled.at(i, g))
                    dve.reciprocal(inv_den[:, :], den[:, :]).then_inc(inv_ready.sem, 1)
                    dve.wait_ge(inv_ready.sem, inv_ready.at(i, g + 1))
                    dve.wait_ge(o_copied.sem, o_copied.at(i, g + 1))
                    dve.tensor_tensor(o_buf[:, :], o_buf[:, :], inv_den[:, :], ALU.mult).then_inc(o_scaled.sem, 1)

                for s in range(STEPS):
                    if with_b:
                        for kind, n in A_AT[s]:
                            a_part(i + 1, kind, n)
                        if s == STATS_AT:
                            dve.wait_ge(x_in.sem, x_in.at(i + 1, DMA))
                            for t in range(TT):
                                dve.bn_stats(stats[:, t, :], x_buf[1 - par][:, t, :]).then_inc(stats1.sem, 1)
                            moments(range(TT), stats1, moments1, i + 1, 0)
                    if with_d and s % TT == TT - 1:
                        add_last_probs(s)
                    if with_d and s >= 5 and (s - 5) % TT == 0:
                        scale_o((s - 5) // TT)
                bank_of = tables[2]
                for kind, n in phase2(with_d, with_b):
                    bank = None if kind in ("B", "DEN") else work[bank_of[kind, n]]
                    if kind == "B":
                        dve.wait_ge(max_ps.sem, max_ps.at(i + 1, n + 1))
                        dve.tensor_reduce(maxima[:, 2 * n:2 * n + 2], scores[n % 2][:, :, :], AX_X, ALU.max)\
                           .then_inc(max_done.sem, 1)
                        if n % (MAX_UNITS // 2) == MAX_UNITS // 2 - 1:
                            half = n // (MAX_UNITS // 2)
                            c = slice(MAX_UNITS * half, MAX_UNITS * (half + 1))
                            dve.wait_ge(max_done.sem, max_done.at(i + 1, n + 1))
                            dve.tensor_scalar(neg_max[:, c], maxima[:, c], -1.0 / MAX_UNIT, None, ALU.mult)\
                               .then_inc(negmax_s.sem, 1)
                    if kind == "DEN":
                        scale_o(n)
                    if kind == "PO":
                        dve.wait_ge(op_ps.sem, op_ps.at(i, n + 1))
                        dve.wait_ge(xbo_ready.sem, xbo_ready.at(i, n + 1))
                        dve.scalar_tensor_tensor(out=x_buf[par][:, n, :], in0=bank[:, :], scalar=UNW,
                                                 in1=x_buf[par][:, n, :], op0=ALU.mult, op1=ALU.add)\
                           .then_inc(x1_ready.sem, 1)
                        dve.wait_ge(x1_ready.sem, x1_ready.at(i, n + 1))
                        dve.bn_stats(stats[:, n, :], x_buf[par][:, n, :]).then_inc(stats2.sem, 1)
                        moments(range(n, n + 1), stats2, moments2, i, MOMENTS * n)
                    if kind == "LG":
                        link = iter(range(1, GATE_A + 1))
                        ops = TT * [None]
                        dve.wait_ge(logit_ps.sem, logit_ps.at(i, 1))
                        dve.scalar_tensor_tensor(
                            out=logits[:, :, :],
                            in0=bank[:, 0:TT * EXPERTS].rearrange("p (t e) -> p t e", t=TT), scalar=UNW,
                            in1=bg_row[:, :].unsqueeze(1).to_broadcast([P, TT, EXPERTS]),
                            op0=ALU.mult, op1=ALU.add).then_inc(gate_a.sem, 1)
                        dve.wait_ge(gate_a.sem, gate_a.at(i, 1))
                        other = logits[:, :, :].unsqueeze(2).to_broadcast([P, TT, EXPERTS, EXPERTS])
                        own = logits[:, :, :].unsqueeze(3).to_broadcast([P, TT, EXPERTS, EXPERTS])
                        tri = lower_tri[:, :, :].unsqueeze(1).to_broadcast([P, TT, EXPERTS, EXPERTS])
                        dve.tensor_reduce(top1[:, :], logits[:, :, :], AX_X, ALU.max).then_inc(gate_a.sem, 1)
                        dve.tensor_tensor(cmp_gt, other, own, ALU.is_gt).then_inc(gate_a.sem, 1)
                        dve.tensor_tensor(cmp_eq, other, own, ALU.is_equal).then_inc(gate_a.sem, 1)
                        dve.wait_ge(gate_a.sem, gate_a.at(i, 4))
                        dve.tensor_tensor(cmp_eq, cmp_eq, tri, ALU.mult).then_inc(gate_a.sem, 1)
                        dve.wait_ge(gate_a.sem, gate_a.at(i, 5))
                        dve.tensor_tensor(cmp_gt, cmp_gt, cmp_eq, ALU.add).then_inc(gate_a.sem, 1)
                        dve.wait_ge(gate_a.sem, gate_a.at(i, 6))
                        dve.tensor_reduce(rank[:, :, :], cmp_gt, AX_X, ALU.add).then_inc(gate_a.sem, 1)
                        dve.tensor_tensor(gap[:, :, :], logits[:, :, :],
                                          top1[:, :].unsqueeze(2).to_broadcast([P, TT, EXPERTS]),
                                          ALU.subtract).then_inc(gate_a.sem, 1)
                    if (kind, n) == ("W1", 1):
                        dve.wait_ge(gate_a.sem, gate_a.at(i, GATE_A))
                        dve.wait_ge(gate_exp_s.sem, gate_exp_s.at(i, 1))
                        dve.scalar_tensor_tensor(out=gates[:, :, :], in0=rank[:, :, :], scalar=2.0,
                                                 in1=gate_exp[:, :, :], op0=ALU.is_lt, op1=ALU.mult)\
                           .then_inc(gate_b.sem, 1)
                        dve.wait_ge(gate_b.sem, gate_b.at(i, 1))
                        dve.tensor_reduce(gate_den[:, 0, :], gates[:, :, :], AX_X, ALU.add).then_inc(gate_b.sem, 1)
                        dve.wait_ge(gate_b.sem, gate_b.at(i, 2))
                        dve.reciprocal(gate_den[:, 1, :], gate_den[:, 0, :]).then_inc(gate_b.sem, 1)
                        dve.wait_ge(gate_b.sem, gate_b.at(i, 3))
                        dve.tensor_tensor(gates[:, :, :], gates[:, :, :],
                                          gate_den[:, 1, :].unsqueeze(2).to_broadcast([P, TT, EXPERTS]),
                                          ALU.mult).then_inc(gate_b.sem, 1)
                        dve.wait_ge(gate_b.sem, gate_b.at(i, 4))
                        dve.tensor_copy(gate_pair[:, :, 0:EXPERTS], gates[:, :, :]).then_inc(gate_b.sem, 1)
                        dve.wait_ge(gate_b.sem, gate_b.at(i, 5))
                        dve.tensor_tensor(gate_pair[:, :, EXPERTS:2 * EXPERTS], gates[:, :, :],
                                          gate_pair[:, :, 0:EXPERTS], ALU.subtract).then_inc(gate_b.sem, 1)
                    if kind == "GB":
                        dve.wait_ge(gbc_ps.sem, gbc_ps.at(i, n + 1))
                        dve.wait_ge(h_ready.sem, h_ready.at(i, n + 1))
                        if n >= 2:
                            dve.wait_ge(gh_lo_s.sem, gh_lo_s.at(i, n - 1))
                        dve.tensor_tensor(gh32[:, n % 2, :], bank[:, :], h_buf[:, n, :], ALU.mult)\
                           .then_inc(gh32_s.sem, 1)
                    if kind == "W2":
                        dve.wait_ge(w2_ps.sem, w2_ps.at(i, n + 1))
                        dve.scalar_tensor_tensor(out=x_buf[par][:, n, :], in0=bank[:, :], scalar=SCALING * UNW,
                                                 in1=x_buf[par][:, n, :], op0=ALU.mult, op1=ALU.add)\
                           .then_inc(out_ready.sem, 1)

            run_steps(dve, step)

        @block.tensor
        def _(pe):
            pe.wait_ge(ln_const.sem, 4)
            pe.wait_ge(setup_hi.sem, SETUP_HI)
            pe.wait_ge(setup_lo.sem, SETUP_LO)

            def three(dst, lhs_hi, lhs_lo, rhs_hi, rhs_lo, tiles=range(DT), of=DT):
                for t in tiles:
                    pe.matmul(dst, lhs_hi(t), rhs_hi(t), start=(t == 0), stop=False)
                    pe.matmul(dst, lhs_hi(t), rhs_lo(t), start=False, stop=False)
                    last = pe.matmul(dst, lhs_lo(t), rhs_hi(t), start=False, stop=(t == of - 1))
                return last

            def project_v(b, n, bank):
                cols = slice(P * n, P * n + P)
                three(bank[:, :], lambda t: ctxT_hi[:, t, cols], lambda t: ctxT_lo[:, t, cols],
                      lambda t: w_hi["v"][:, t, :], lambda t: w_lo["v"][:, t, :]).then_inc(v_ps.sem, 1)

            def free(i, prior):
                if prior is None:
                    return
                kind, n, offset = prior
                sem = bank_read[kind]
                pe.wait_ge(sem.sem, sem.at(i + offset, n + 1))

            def a_part(i, kind, n, prior):
                b = i + 1
                free(i, prior[kind, n])
                bank = work[BANK_A[kind, n]]
                cols = slice(P * n, P * n + P)
                if kind == "CT":
                    if n == 0:
                        pe.wait_ge(ctx_in.sem, ctx_in.at(b, DMA))
                    for t in range(DT):
                        last = pe.transpose(bank[:, P * t:P * t + P], ctx_buf[:, n, P * t:P * t + P], ident32[:, :])
                    last.then_inc(ctxT_ps.sem, 1)
                if kind == "XT":
                    pe.wait_ge(xn_ready.sem, xn_ready.at(b, n + 1))
                    for t in range(DT):
                        last = pe.transpose(bank[:, P * t:P * t + P], xn[:, n, P * t:P * t + P], ident32[:, :])
                    last.then_inc(xT_ps.sem, 1)
                if kind == "Q":
                    if n == 0:
                        pe.wait_ge(xT_lo_s.sem, xT_lo_s.at(b, TT))
                    three(bank[:, :], lambda t: w_hi["q"][:, t, cols], lambda t: w_lo["q"][:, t, cols],
                          lambda t: xT_hi[:, t, :], lambda t: xT_lo[:, t, :]).then_inc(q_ps.sem, 1)
                if kind == "K":
                    if n == 0:
                        pe.wait_ge(ctxT_lo_s.sem, ctxT_lo_s.at(b, TT))
                    three(bank[:, :], lambda t: w_hi["k"][:, t, cols], lambda t: w_lo["k"][:, t, cols],
                          lambda t: ctxT_hi[:, t, :], lambda t: ctxT_lo[:, t, :]).then_inc(k_ps.sem, 1)
                if kind == "V":
                    project_v(b, n, bank)

            def step(i, par, tables, with_d, with_b):
                prior_a, (oT_prior, den_prior), bank_of, prior_d, _ = tables

                def score_step(s):
                    g, kt = s // TT, s % TT
                    if s == 0:
                        pe.wait_ge(maxrow_in[0].sem, maxrow_in[0].at(i, DMA))
                    if s == STEPS // 2:
                        pe.wait_ge(maxrow_in[1].sem, maxrow_in[1].at(i, DMA))
                    for pr in range(2):
                        if s >= 1:
                            pe.wait_ge(exp_done.sem, exp_done.at(i, 2 * s - 1 + pr))
                        else:
                            pe.wait_ge(max_done.sem, max_done.at(i, MAX_UNITS - 1 + pr))
                        for j in range(2):
                            h = HT * g + 2 * pr + j
                            last = pe.matmul(scores[pr][:, j, :], k_stack[0:STACK + 1, h, P * kt:P * kt + P],
                                             q_stack[0:STACK + 1, h, :], start=True, stop=True)
                        last.then_inc(score_ps.sem, 1)

                def values_step(s):
                    g, kt = s // TT, s % TT
                    if s == 0:
                        free(i, oT_prior)
                        pe.wait_ge(v_ready.sem, v_ready.at(i, TT))
                    elif kt == 0:
                        pe.wait_ge(o_copied.sem, o_copied.at(i, g))
                    pe.wait_ge(exp_done.sem, exp_done.at(i, 2 * s + 2))
                    for j in range(HT):
                        h = HT * g + j
                        last = pe.matmul(oT[DK * j:DK * j + DK, :], v_buf[par][:, kt, DK * h:DK * h + DK],
                                         probs[s % RING][:, j, :], start=(kt == 0), stop=(kt == TT - 1))
                    last.then_inc(pv_done.sem, 1)

                def denominators(g):
                    if g == 0:
                        free(i, den_prior)
                    else:
                        pe.wait_ge(inv_ready.sem, inv_ready.at(i, g))
                    pe.wait_ge(sum_dve.sem, sum_dve.at(i, g + 1))
                    for j in range(HT):
                        last = pe.matmul(den[DK * j:DK * j + DK, :], ones[:, :], prob_sum[:, j, :],
                                         start=True, stop=True)
                    last.then_inc(den_ps.sem, 1)

                for s in range(STEPS):
                    if with_d:
                        score_step(s)
                    if with_b:
                        for kind, n in A_AT[s]:
                            a_part(i, kind, n, prior_a)
                    if with_d and s >= 1:
                        values_step(s - 1)
                    if with_d and s >= 5 and (s - 5) % TT == 0:
                        denominators((s - 5) // TT)
                if with_d:
                    values_step(STEPS - 1)

                for kind, n in phase2(with_d, with_b):
                    if kind == "B":
                        h, qt = n // 2, 2 * (n % 2)
                        if n == 0:
                            pe.wait_ge(stack_in[0].sem, stack_in[0].at(i + 1, 24 * DMA))
                            if with_d:
                                pe.wait_ge(exp_done.sem, exp_done.at(i, 2 * STEPS))
                        if n == MAX_UNITS // 2:
                            pe.wait_ge(stack_in[1].sem, stack_in[1].at(i + 1, 24 * DMA))
                        if n >= 2:
                            pe.wait_ge(max_done.sem, max_done.at(i + 1, n - 1))
                        for j in range(2):
                            q = P * (qt + j)
                            last = pe.matmul(scores[n % 2][:, j, :], q_stack[0:STACK, h, q:q + P],
                                             k_stack[0:STACK, h, :], start=True, stop=True)
                        last.then_inc(max_ps.sem, 1)
                        continue
                    if kind == "DEN":
                        denominators(n)
                        continue
                    if kind != "PO":
                        free(i, prior_d[kind, n])
                    bank = work[bank_of[kind, n]]
                    cols = slice(P * n, P * n + P)
                    if kind == "MT":
                        pe.wait_ge(negmax_s.sem, negmax_s.at(i + 1, n + 1))
                        pe.transpose(bank[:, :].bitcast(F16)[0:MAX_UNITS, 0:P],
                                     neg_max[:, MAX_UNITS * n:MAX_UNITS * (n + 1)], ident16[:, :])\
                          .then_inc(maxT_ps.sem, 1)
                    if kind in ("OP", "PO"):
                        if n == 0:
                            pe.wait_ge(o_lo_s.sem, o_lo_s.at(i, GROUPS if kind == "PO" else GROUPS - 1))
                        last = three(bank[:, :], lambda t: o_hi[:, t, cols], lambda t: o_lo[:, t, cols],
                                     lambda t: w_hi["o"][:, t, :], lambda t: w_lo["o"][:, t, :],
                                     range(GROUPS - 1, GROUPS) if kind == "PO" else range(GROUPS - 1), GROUPS)
                        if kind == "PO":
                            last.then_inc(op_ps.sem, 1)
                    if kind == "V":
                        project_v(i + 1, n, bank)
                    if kind == "T":
                        pe.wait_ge(x1n_ready.sem, x1n_ready.at(i, n + 1))
                        for t in range(DT):
                            last = pe.transpose(bank[:, P * t:P * t + P], xn[:, n, P * t:P * t + P], ident32[:, :])
                        last.then_inc(x1T_ps.sem, 1)
                    if kind == "LG":
                        pe.wait_ge(x1T_lo_s.sem, x1T_lo_s.at(i, TT))
                        for m in range(TT):
                            tok = slice(P * m, P * m + P)
                            last = three(bank[:, EXPERTS * m:EXPERTS * (m + 1)],
                                         lambda t: xT_hi[:, t, tok], lambda t: xT_lo[:, t, tok],
                                         lambda t: wg_hi[:, t, :], lambda t: wg_lo[:, t, :])
                        last.then_inc(logit_ps.sem, 1)
                    if kind == "W1":
                        three(bank[:, :], lambda t: w_hi["1"][:, t, cols], lambda t: w_lo["1"][:, t, cols],
                              lambda t: xT_hi[:, t, :], lambda t: xT_lo[:, t, :]).then_inc(w1_ps.sem, 1)
                    if kind == "GT":
                        pe.wait_ge(gate_b.sem, gate_b.at(i, GATE_B))
                        for m in range(TT):
                            last = pe.transpose(bank[:, :].bitcast(F16)[0:2 * EXPERTS, P * m:P * m + P],
                                                gate_pair[:, m, :], ident16[:, :])
                        last.then_inc(gateT_ps.sem, 1)
                    if kind == "GB":
                        if n == 0:
                            pe.wait_ge(gateT_s.sem, gateT_s.at(i, 1))
                        pe.matmul(bank[:, :], select16[:, n, :], gateT[:, :], start=True, stop=True)\
                          .then_inc(gbc_ps.sem, 1)
                    if kind == "W2":
                        if n == 0:
                            pe.wait_ge(gh_lo_s.sem, gh_lo_s.at(i, DT))
                        three(bank[:, :], lambda t: gh_hi[:, t, cols], lambda t: gh_lo[:, t, cols],
                              lambda t: w_hi["2"][:, t, :], lambda t: w_lo["2"][:, t, :]).then_inc(w2_ps.sem, 1)

            three(work[0][:, :], lambda t: bv_hi[:, t:t + 1].to_broadcast([P, P]),
                  lambda t: bv_lo[:, t:t + 1].to_broadcast([P, P]),
                  lambda t: w_hi["o"][:, t, :], lambda t: w_lo["o"][:, t, :]).then_inc(bo_ps.sem, 1)
            pe.wait_ge(bo_ready.sem, 1)
            run_steps(pe, step)


def kernel(**inputs):
    import concourse.bacc as _bacc
    from concourse.bass_utils import run_bass_kernel_spmd as _run

    def flip(name):
        a = np.asarray(inputs[name])
        return np.ascontiguousarray(a.reshape(-1, a.shape[-1]).T)

    def by_partition(name):
        return np.ascontiguousarray(np.asarray(inputs[name]).reshape(-1, P).T)

    w2 = np.asarray(inputs["L0_ffn_W2"])
    experts = w2.shape[0]
    er = experts * w2.shape[2]
    select = np.zeros((2 * experts, er), np.float32)
    for e in range(experts):
        select[[e, experts + e], e * (er // experts):(e + 1) * (er // experts)] = 1.0
    arrays = {
        "x": inputs["x"], "ctx": inputs["ctx_1024"],
        "wq_t": flip("L0_xattn_Wq"), "bq": by_partition("L0_xattn_bq"),
        "wk_t": flip("L0_xattn_Wk"), "bk": by_partition("L0_xattn_bk"),
        "wv_t": flip("L0_xattn_Wv"), "bv": by_partition("L0_xattn_bv"),
        "wo_t": flip("L0_xattn_Wo"), "bo": inputs["L0_xattn_bo"],
        "wg_t": flip("L0_ffn_Wg"), "bg": inputs["L0_ffn_bg"],
        "w1_t": flip("L0_ffn_W1"),
        "w2_t": np.ascontiguousarray(w2.transpose(0, 2, 1).reshape(er, w2.shape[1])),
        "ident": np.eye(P, dtype=np.float32), "select": select,
        "lower": np.tril(np.ones((experts, experts), np.float32), -1),
    }
    arrays = {n: np.ascontiguousarray(a) for n, a in arrays.items()}
    nc = _bacc.Bacc("TRN2", target_bir_lowering=False, num_devices=1, dynamic_dma_scratch_size=4096)
    args = [nc.dram_tensor(n, a.shape, mybir.dt.from_np(a.dtype), kind="ExternalInput").ap()
            for n, a in arrays.items()]
    out = nc.dram_tensor("out", arrays["x"].shape, F32, kind="ExternalOutput").ap()
    xattn_moe_kernel(nc, *args, out)
    r = _run(nc, [arrays], core_ids=[0])
    return r.results[0]["out"]
```

```python
from contextlib import ExitStack

from concourse import mybir
import numpy as np

F32 = mybir.dt.float32
F16 = mybir.dt.float16
ALU = mybir.AluOpType
ACT = mybir.ActivationFunctionType
AX_X = mybir.AxisListType.X

P = 128
HEADS = 16
DK = 32
EXPERTS = 8
LN_EPS = 1e-5
SCALE_W = 64.0
MAX_UNIT = SCALE_W * SCALE_W
SCALING = 2.0
DMA = 16


class Count:

    def __init__(self, sem, per):
        self.sem, self.per = sem, per

    def at(self, b, n):
        return b * self.per + n


def xattn_moe_kernel(nc, x, ctx, wq_t, bq, wk_t, bk, wv_t, bv, wo_t, bo, wg_t, bg, w1_t, w2_t,
                     ident, select, lower, out):
    B, T, D = x.shape
    TT = T // P
    DT = D // P
    HT = P // DK
    GROUPS = HEADS // HT
    EXP_SCALE = 1.0 / (MAX_UNIT * float(np.sqrt(np.float32(DK))))
    UNW = 1.0 / SCALE_W
    STACK = 3 * DK
    MAX_UNITS = HEADS * TT // 2
    RING = 3
    LN_STEPS = 8

    with ExitStack() as st:
        def sb(name, shape, dt):
            return st.enter_context(nc.sbuf_tensor(name, shape, dt))

        def pb(name, shape, dt):
            return st.enter_context(nc.psum_tensor(name, shape, dt))

        def count(name, per):
            return Count(st.enter_context(nc.semaphore(name)), per)

        w_hi = {n: sb(f"w{n}_hi", [P, DT, D], F16) for n in ("k", "q", "v", "o", "1", "2")}
        w_lo = {n: sb(f"w{n}_lo", [P, DT, D], F16) for n in ("k", "q", "v", "o", "1", "2")}
        wg_hi = sb("wg_hi", [P, DT, EXPERTS], F16)
        wg_lo = sb("wg_lo", [P, DT, EXPERTS], F16)
        bq_col = sb("bq_col", [P, DT], F32)
        bk_col = sb("bk_col", [P, DT], F32)
        bv_col = sb("bv_col", [P, DT], F32)
        bv_hi = sb("bv_hi", [P, DT], F16)
        bv_lo = sb("bv_lo", [P, DT], F16)
        bo_row = sb("bo_row", [P, D], F32)
        bg_row = sb("bg_row", [P, EXPERTS], F32)
        ident32 = sb("ident32", [P, P], F32)
        ident16 = sb("ident16", [P, P], F16)
        select16 = sb("select16", [2 * EXPERTS, DT, P], F16)
        lower_tri = sb("lower_tri", [P, EXPERTS, EXPERTS], F32)
        ones = sb("ones", [P, DK], F32)
        table_probe = sb("table_probe", [P, 1], F32)
        minus_half = sb("minus_half", [P, TT], F32)
        three_halves = sb("three_halves", [P, TT], F32)

        x_buf = [sb(f"x_buf{p}", [P, TT, D], F32) for p in range(2)]
        ctx_buf = sb("ctx_buf", [P, TT, D], F32)
        xn = sb("xn", [P, TT, D], F32)
        ctxT_hi = sb("ctxT_hi", [P, DT, T], F16)
        ctxT_lo = sb("ctxT_lo", [P, DT, T], F16)
        xT_hi = sb("xT_hi", [P, DT, T], F16)
        xT_lo = sb("xT_lo", [P, DT, T], F16)
        q_hi = sb("q_hi", [P, DT, T], F16)
        q_lo = sb("q_lo", [P, DT, T], F16)
        k_hi = sb("k_hi", [P, DT, T], F16)
        k_lo = sb("k_lo", [P, DT, T], F16)
        q_stack = sb("q_stack", [P, HEADS, T], F16)
        k_stack = sb("k_stack", [P, HEADS, T], F16)
        v_buf = [sb(f"v_buf{p}", [P, TT, D], F32) for p in range(2)]
        shared = sb("shared", [P, (RING + 1) * HT * T], F32)
        probs = [shared[:, s * HT * T:(s + 1) * HT * T].rearrange("p (j q) -> p j q", j=HT)
                 for s in range(RING)]
        prob_sum = shared[:, RING * HT * T:(RING + 1) * HT * T].rearrange("p (j q) -> p j q", j=HT)
        h_buf = probs[0]
        gh_hi = shared[:, HT * T:HT * T + HT * T // 2].bitcast(F16).rearrange("p (j q) -> p j q", j=HT)
        gh_lo = shared[:, HT * T + HT * T // 2:2 * HT * T].bitcast(F16).rearrange("p (j q) -> p j q", j=HT)
        gh32 = probs[2][:, 0:2, :]
        x1T32 = probs[2][:, 2:4, :]
        expert_out = x1T32
        cmp_gt = prob_sum[:, 0, 0:TT * EXPERTS * EXPERTS].rearrange("p (t e j) -> p t e j", t=TT, e=EXPERTS)
        cmp_eq = prob_sum[:, 1, 0:TT * EXPERTS * EXPERTS].rearrange("p (t e j) -> p t e j", t=TT, e=EXPERTS)
        stage = [shared[:, n * DT * D:(n + 1) * DT * D].rearrange("p (t d) -> p t d", t=DT) for n in range(RING + 1)]

        o_buf = sb("o_buf", [P, T], F32)
        inv_den = sb("inv_den", [P, T], F32)
        o_hi = sb("o_hi", [P, DT, T], F16)
        o_lo = sb("o_lo", [P, DT, T], F16)
        maxima = sb("maxima", [P, HEADS * TT], F32)
        neg_max = sb("neg_max", [P, HEADS * TT], F16)
        max_rows = sb("max_rows", [HEADS * TT // 2, 2, P], F16)
        stats = sb("stats", [P, TT, 6], F32)
        moment_tmp = sb("moment_tmp", [P, 4, TT], F32)
        ln_tmp = sb("ln_tmp", [P, 8, TT], F32)
        logits = sb("logits", [P, TT, EXPERTS], F32)
        top1 = sb("top1", [P, TT], F32)
        rank = sb("rank", [P, TT, EXPERTS], F32)
        gap = sb("gap", [P, TT, EXPERTS], F32)
        gate_exp = sb("gate_exp", [P, TT, EXPERTS], F32)
        gate_den = sb("gate_den", [P, 2, TT], F32)
        gates = sb("gates", [P, TT, EXPERTS], F32)
        gate_pair = sb("gate_pair", [P, TT, 2 * EXPERTS], F16)
        gateT = sb("gateT", [2 * EXPERTS, T], F16)

        scores = [pb(f"scores{n}", [P, 2, T], F32) for n in range(2)]
        work = [pb(f"work{n}", [P, T], F32) for n in range(4)]
        oT, den = work[2], work[3]

        const_in = count("const_in", 0)
        stage_in = [count(f"stage_in{n}", 0) for n in range(RING + 1)]
        ln_const = count("ln_const", 0)
        ones_set = count("ones_set", 0)
        setup_hi = count("setup_hi", 0)
        setup_lo = count("setup_lo", 0)
        SETUP = 5
        bo_ps = count("bo_ps", 0)
        bo_ready = count("bo_ready", 0)
        x_in = count("x_in", DMA)
        ctx_in = count("ctx_in", DMA)
        stack_in = [count(f"stack_in{n}", 24 * DMA) for n in range(2)]
        maxrow_in = [count(f"maxrow_in{n}", DMA) for n in range(2)]
        out_stored = count("out_stored", TT * DMA)
        stats1 = count("stats1", TT)
        MOMENTS = 6
        moments1 = count("moments1", MOMENTS)
        ln1_step = count("ln1_step", LN_STEPS)
        xn_ready = count("xn_ready", TT)
        xbo_ready = count("xbo_ready", TT)
        ctxT_ps = count("ctxT_ps", TT)
        ctxT_hi_s = count("ctxT_hi_s", TT)
        ctxT_lo_s = count("ctxT_lo_s", TT)
        xT_ps = count("xT_ps", TT)
        xT_hi_s = count("xT_hi_s", TT)
        xT_lo_s = count("xT_lo_s", TT)
        q_ps = count("q_ps", DT)
        q_hi_s = count("q_hi_s", DT)
        q_lo_s = count("q_lo_s", DT)
        k_ps = count("k_ps", DT)
        k_hi_s = count("k_hi_s", DT)
        k_lo_s = count("k_lo_s", DT)
        v_ps = count("v_ps", TT)
        v_ready = count("v_ready", TT)
        max_ps = count("max_ps", MAX_UNITS)
        max_done = count("max_done", MAX_UNITS)
        negmax_s = count("negmax_s", 2)
        maxT_ps = count("maxT_ps", 2)
        maxrow_s = count("maxrow_s", 2)
        STEPS = GROUPS * TT
        score_ps = count("score_ps", 2 * STEPS)
        exp_done = count("exp_done", 2 * STEPS)
        pv_done = count("pv_done", STEPS)
        SUMS = (TT - 1) * GROUPS - 1
        sum_pool = count("sum_pool", SUMS)
        sum_dve = count("sum_dve", SUMS)
        den_ps = count("den_ps", GROUPS)
        o_copied = count("o_copied", GROUPS)
        inv_ready = count("inv_ready", GROUPS)
        o_scaled = count("o_scaled", GROUPS)
        o_hi_s = count("o_hi_s", GROUPS)
        o_lo_s = count("o_lo_s", GROUPS)
        op_ps = count("op_ps", TT)
        x1_ready = count("x1_ready", TT)
        stats2 = count("stats2", TT)
        moments2 = count("moments2", MOMENTS * TT // 2)
        ln2_step = count("ln2_step", LN_STEPS * TT // 2)
        x1n_ready = count("x1n_ready", TT)
        x1T_ps = count("x1T_ps", TT)
        x1T_hi_s = count("x1T_hi_s", TT)
        x1T_copied = count("x1T_copied", TT)
        x1T_lo_s = count("x1T_lo_s", TT)
        logit_ps = count("logit_ps", 1)
        GATE_A, GATE_B = 8, 6
        gate_a = count("gate_a", GATE_A)
        gate_exp_s = count("gate_exp_s", 1)
        gate_b = count("gate_b", GATE_B)
        gateT_ps = count("gateT_ps", 1)
        gateT_s = count("gateT_s", 1)
        w1_ps = count("w1_ps", DT)
        h_ready = count("h_ready", DT)
        gbc_ps = count("gbc_ps", DT)
        gh32_s = count("gh32_s", DT)
        gh_hi_s = count("gh_hi_s", DT)
        gh_lo_s = count("gh_lo_s", DT)
        w2_ps = count("w2_ps", TT)
        w2_copied = count("w2_copied", TT)
        out_ready = count("out_ready", TT)

        bank_read = {"CT": ctxT_lo_s, "XT": xT_lo_s, "Q": q_lo_s, "K": k_lo_s, "V": v_ready,
                     "MT": maxrow_s, "OP": x1_ready, "T": x1T_copied, "LG": gate_a, "W1": h_ready,
                     "GT": gateT_s, "GB": gh32_s, "W2": w2_copied, "O": o_copied, "DEN": inv_ready}

        def first_uses(order):
            return list(dict.fromkeys((k.rstrip("h"), n) for k, n in order))

        A_AT = [[(u.rstrip("h")[:-1] + "h" * u.endswith("h"), int(u.rstrip("h")[-1])) for u in step.split()]
                for step in (
                    "CT0 CT1 CT2 CT3", "", "K0", "", "K1", "K2h", "K2 XT0", "XT1", "XT2 XT3", "K3", "Q0", "Q1h Q1",
                    "", "Q2h", "Q2 Q3h", "Q3")]
        A_ORDER = [u for step in A_AT for u in step]
        A_USES = first_uses(A_ORDER)
        STATS_AT, INV_AT, NORM_AT, BO_AT = 2, 3, [4, 5, 6, 6], 8
        DEN_AT, OHI_AT, OLO_AT = 4, 7, 7
        PHASE2 = ("V0h@0 B B DEN3 V0 B B V1@1 OP0@2 OP1@0 B PO0 PO1 OP2@3 B PO2 OP3@1 PO3 B V2h@0 B B V2 "
                  "T0@2 T1@3 B B V3h@0 T2@1 B T3@3 B V3 B B LG0@3 W1_0h@1 W1_0 B W1_1@2 B B GT0@1 W1_2h@0 "
                  "MT0@3 B GB0@2 GB1@3 B W1_2 B W1_3h@1 B W1_3 B GB2@0 B W2_0h@2 B W2_1h@3 GB3@1 B W2_2h@0 "
                  "B B W2_0 B W2_1 B W2_2 B B W2_3h@1 W2_3 MT1@2").split()
        BANK_2 = {}

        def phase2(with_d, with_b):
            steps, units = [], 0
            for s in PHASE2:
                name, _, bank = s.partition("@")
                half = name[-1] == "h"
                name = name.rstrip("h")
                kind, n = name.split("_") if "_" in name else (name.rstrip("0123456789"), name[-1])
                kind += "h" * half
                if bank:
                    BANK_2[kind.rstrip("h"), int(n)] = int(bank)
                if kind == "B":
                    if with_b:
                        steps.append(("B", units))
                    units += 1
                elif with_b if kind in ("MT", "V", "Vh") else with_d:
                    steps.append((kind, int(n)))
            assert units == MAX_UNITS, units
            return steps

        def d_uses(with_d, with_b):
            return first_uses([u for u in phase2(with_d, with_b) if (u[0].rstrip("h"), u[1]) in BANK_2])

        BANK_A = {u: n % 2 for n, u in enumerate(A_USES)}

        def prior_uses(uses, bank_of, before):
            last, prior = dict(before), {}
            for kind, n, offset in uses:
                prior[kind, n] = last.get(bank_of[kind, n])
                last[bank_of[kind, n]] = (kind, n, offset)
            return prior, last

        def bank_tables(with_d, with_b, before):
            first, last = {}, dict(before)
            if with_b:
                first, last = prior_uses([(k, n, 1) for k, n in A_USES], BANK_A, last)
            if with_d:
                oT_prior, den_prior = last.get(2), last.get(3)
                last[2], last[3] = ("O", GROUPS - 1, 0), ("DEN", GROUPS - 1, 0)
            else:
                oT_prior = den_prior = None
            uses = d_uses(with_d, with_b)
            bank_of = {**BANK_2, **{("PO", n): bank for (k, n), bank in BANK_2.items() if k == "OP"}}
            second, last = prior_uses([(k, n, 1 if k in ("MT", "V") else 0) for k, n in uses], bank_of, last)
            return first, (oT_prior, den_prior), bank_of, second, last

        def shifted(last):
            return {bank: (k, n, offset - 1) for bank, (k, n, offset) in last.items()}

        PROLOGUE = bank_tables(False, True, {})
        FIRST = bank_tables(True, True, shifted(PROLOGUE[4]))
        MIDDLE = bank_tables(True, True, shifted(FIRST[4]))
        assert shifted(MIDDLE[4]) == shifted(FIRST[4])
        LAST = bank_tables(True, False, shifted(MIDDLE[4]))

        def run_steps(engine, step):
            step(-1, 1, PROLOGUE, False, True)
            step(0, 0, FIRST, True, True)
            with engine.Fori(1, B - 3, 2) as i:
                step(i, 1, MIDDLE, True, True)
                step(i + 1, 0, MIDDLE, True, True)
            step(B - 3, 1, MIDDLE, True, True)
            step(B - 2, 0, MIDDLE, True, True)
            step(B - 1, 1, LAST, True, False)

        x_tiles = x.rearrange("b (t p) d -> b p t d", p=P)
        ctx_tiles = ctx.rearrange("b (t p) d -> b p t d", p=P)
        out_tiles = out.rearrange("b (t p) d -> b t p d", p=P)
        weights = [("k", wk_t), ("q", wq_t), ("v", wv_t), ("o", wo_t), ("1", w1_t), ("2", w2_t)]
        SPLIT_AT = {1: 1, 3: 2, 5: 3, 7: 4, 9: 5}
        STAGES = len(stage)

        def add_probs(engine, i, s, heads, sums):
            g, kt = s // TT, s % TT
            engine.wait_ge(exp_done.sem, exp_done.at(i, 2 * s + 2))
            if kt == 1 and g >= 1:
                engine.wait_ge(den_ps.sem, den_ps.at(i, g))
            if kt >= 2:
                engine.wait_ge(sums.sem, sums.at(i, (TT - 1) * g + kt - 1))
            before = probs[(s - 1) % RING] if kt == 1 else prob_sum
            engine.tensor_tensor(prob_sum[:, heads, :], before[:, heads, :], probs[s % RING][:, heads, :],
                                 ALU.add).then_inc(sums.sem, 1)

        block = st.enter_context(nc.Block())

        @block.sync
        def _(sp):
            def stack(b, half, hi, lo, hi_s, lo_s, dst, order):
                sp.wait_ge(hi_s.sem, hi_s.at(b, 2 * half + 2))
                sp.wait_ge(lo_s.sem, lo_s.at(b, 2 * half + 2))
                for g, part in enumerate(order):
                    src = hi if part == "hi" else lo
                    for j in range(HT):
                        heads = dst[DK * g:DK * g + DK, :, :].rearrange("p (t j) q -> p t j q", j=HT)
                        sp.dma_start(heads[:, 2 * half:2 * half + 2, j, :],
                                     src[DK * j:DK * j + DK, 2 * half:2 * half + 2, :])\
                          .then_inc(stack_in[half].sem, DMA)

            def step(i, par, tables, with_d, with_b):
                if with_d and with_b:
                    if not (isinstance(i, int) and i == 0):
                        sp.wait_ge(out_stored.sem, out_stored.at(i - 1, TT * DMA))
                    sp.dma_start(x_buf[1 - par][:, :, :], x_tiles[i + 1]).then_inc(x_in.sem, DMA)
                if with_b:
                    for half in range(2):
                        if with_d:
                            sp.wait_ge(score_ps.sem, score_ps.at(i, STEPS * (half + 1)))
                        stack(i + 1, half, k_hi, k_lo, k_hi_s, k_lo_s, k_stack, ("hi", "lo", "hi"))
                        stack(i + 1, half, q_hi, q_lo, q_hi_s, q_lo_s, q_stack, ("hi", "hi", "lo"))
                        if half == 0 and not (isinstance(i, int) and i + 2 >= B):
                            sp.wait_ge(ctxT_ps.sem, ctxT_ps.at(i + 1, TT))
                            sp.dma_start(ctx_buf[:, :, :], ctx_tiles[i + 2]).then_inc(ctx_in.sem, DMA)
                for kind, n in phase2(with_d, with_b):
                    if kind == "MT":
                        sp.wait_ge(maxrow_s.sem, maxrow_s.at(i + 1, n + 1))
                        half_heads = HEADS // 2
                        sp.dma_start(
                            q_stack[STACK:STACK + 1, half_heads * n:half_heads * (n + 1), :],
                            max_rows[:, n, :]).then_inc(maxrow_in[n].sem, DMA)
                    if kind == "W2":
                        sp.wait_ge(out_ready.sem, out_ready.at(i, n + 1))
                        sp.dma_start(out_tiles[i, n], x_buf[par][:, n, :]).then_inc(out_stored.sem, DMA)

            sp.dma_start(ctx_buf[:, :, :], ctx_tiles[0]).then_inc(ctx_in.sem, DMA)
            sp.dma_start(ident32[:, :], ident).then_inc(const_in.sem, DMA)
            sp.dma_start(bq_col[:, :], bq).then_inc(const_in.sem, DMA)
            sp.dma_start(bk_col[:, :], bk).then_inc(const_in.sem, DMA)
            sp.dma_start(bv_col[:, :], bv).then_inc(const_in.sem, DMA)
            sp.dma_start(bo_row[:, :], bo.partition_broadcast(P)).then_inc(const_in.sem, DMA)
            sp.dma_start(bg_row[:, :], bg.partition_broadcast(P)).then_inc(const_in.sem, DMA)
            sp.dma_start(lower_tri[:, :, :], lower.partition_broadcast(P)).then_inc(const_in.sem, DMA)
            sp.dma_start(o_buf[:, 0:DT * EXPERTS].rearrange("p (t e) -> p t e", t=DT),
                         wg_t.rearrange("(t p) e -> p t e", p=P))\
              .then_inc(const_in.sem, DMA)
            sp.dma_start(inv_den[0:2 * EXPERTS, :], select).then_inc(const_in.sem, DMA)
            for n, (_, w) in enumerate(weights):
                if n >= STAGES:
                    sp.wait_ge(setup_lo.sem, SETUP + n - STAGES)
                sp.dma_start(stage[n % STAGES], w.rearrange("(t p) d -> p t d", p=P))\
                  .then_inc(stage_in[n % STAGES].sem, DMA)
                if n == 0:
                    sp.dma_start(x_buf[0][:, :, :], x_tiles[0]).then_inc(x_in.sem, DMA)
            run_steps(sp, step)
            sp.wait_ge(out_stored.sem, out_stored.at(B, 0))

        @block.gpsimd
        def _(pool):
            pool.memset(minus_half[:, :], -0.5).then_inc(ln_const.sem, 1)
            pool.memset(three_halves[:, :], 1.5).then_inc(ln_const.sem, 1)
            pool.wait_ge(ln_const.sem, 2)
            pool.memset(k_stack[STACK:STACK + 1, :, :], MAX_UNIT).then_inc(ln_const.sem, 1)

            def inv_std(b, tiles, base, step_s):
                c = slice(tiles[0], tiles[-1] + 1)
                mean2, var, first, sq, half, factor, inv, neg = (ln_tmp[:, n, c] for n in range(8))
                mh, th = minus_half[:, c], three_halves[:, c]
                for n, (dst, lhs, rhs, op) in enumerate([
                        (first, var, mh, ALU.pow), (sq, first, first, ALU.mult), (half, sq, var, ALU.mult),
                        (half, half, mh, ALU.mult), (factor, half, th, ALU.add), (inv, first, factor, ALU.mult),
                        (neg, mean2, inv, ALU.mult), (neg, neg, mh, ALU.mult)]):
                    if n:
                        pool.wait_ge(step_s.sem, step_s.at(b, base + n))
                    pool.tensor_tensor(dst, lhs, rhs, op).then_inc(step_s.sem, 1)

            def add_bo(b, par):
                pool.wait_ge(xn_ready.sem, xn_ready.at(b, TT))
                for t in range(TT):
                    pool.tensor_tensor(x_buf[par][:, t, :], x_buf[par][:, t, :], bo_row[:, :], ALU.add)\
                        .then_inc(xbo_ready.sem, 1)

            def step(i, par, tables, with_d, with_b):
                for s in range(STEPS):
                    if with_d and s % TT and s < STEPS - 1:
                        add_probs(pool, i, s, slice(0, HT // 2), sum_pool)
                    if with_b and s == INV_AT:
                        pool.wait_ge(moments1.sem, moments1.at(i + 1, MOMENTS))
                        inv_std(i + 1, range(TT), 0, ln1_step)
                    if with_d and s >= OLO_AT and (s - OLO_AT) % TT == 0:
                        o_low(i, (s - OLO_AT) // TT)
                    if with_d and with_b and s == BO_AT:
                        add_bo(i + 1, 1 - par)
                if not with_d:
                    pool.wait_ge(bo_ready.sem, 1)
                    add_bo(i + 1, 1 - par)
                for kind, n in phase2(with_d, with_b):
                    if kind == "DEN":
                        o_low(i, n)
                    if kind == "PO" and n % 2:
                        pool.wait_ge(moments2.sem, moments2.at(i, MOMENTS * (n // 2 + 1)))
                        inv_std(i, range(n - 1, n + 1), LN_STEPS * (n // 2), ln2_step)
                    if kind == "T":
                        pool.wait_ge(x1T_hi_s.sem, x1T_hi_s.at(i, n + 1))
                        pool.wait_ge(x1T_copied.sem, x1T_copied.at(i, n + 1))
                        cols = slice(P * n, P * n + P)
                        pool.tensor_tensor(xT_lo[:, :, cols],
                                           x1T32[:, n % 2, :].rearrange("p (t c) -> p t c", t=DT),
                                           xT_hi[:, :, cols], ALU.subtract).then_inc(x1T_lo_s.sem, 1)
                    if kind == "W2":
                        pool.wait_ge(w2_copied.sem, w2_copied.at(i, n + 1))
                        pool.tensor_tensor(x_buf[par][:, n, :], x_buf[par][:, n, :], expert_out[:, n % 2, :],
                                           ALU.add).then_inc(out_ready.sem, 1)
                    if kind == "GB":
                        pool.wait_ge(gh_hi_s.sem, gh_hi_s.at(i, n + 1))
                        pool.tensor_tensor(gh_lo[:, n, :], gh32[:, n % 2, :], gh_hi[:, n, :], ALU.subtract)\
                            .then_inc(gh_lo_s.sem, 1)

            def o_low(i, g):
                pool.wait_ge(o_hi_s.sem, o_hi_s.at(i, g + 1))
                pool.tensor_tensor(o_lo[:, g, :], o_buf[:, :], o_hi[:, g, :], ALU.subtract)\
                    .then_inc(o_lo_s.sem, 1)

            pool.wait_ge(ln_const.sem, 3)
            run_steps(pool, step)

        @block.scalar
        def _(act):
            def split_high(n):
                name = weights[n][0]
                act.wait_ge(stage_in[n % STAGES].sem, DMA * (n // STAGES + 1))
                act.activation(w_hi[name][:, :, :], stage[n % STAGES], ACT.Copy, scale=SCALE_W)\
                   .then_inc(setup_hi.sem, 1)

            act.wait_ge(const_in.sem, 9 * DMA)
            act.activation(wg_hi[:, :, :], o_buf[:, 0:DT * EXPERTS].rearrange("p (t e) -> p t e", t=DT),
                           ACT.Copy, scale=SCALE_W).then_inc(setup_hi.sem, 1)
            act.activation(ident16[:, :], ident32[:, :], ACT.Copy).then_inc(setup_hi.sem, 1)
            act.activation(select16[:, :, :], inv_den[0:2 * EXPERTS, :].rearrange("p (t c) -> p t c", t=DT),
                           ACT.Copy).then_inc(setup_hi.sem, 1)
            act.activation(bv_hi[:, :], bv_col[:, :], ACT.Copy).then_inc(setup_hi.sem, 1)
            split_high(0)
            act.wait_ge(setup_lo.sem, SETUP)

            def copy_v(b, par, n, bank):
                act.wait_ge(v_ps.sem, v_ps.at(b, n + 1))
                act.activation(v_buf[par][:, n, :], bank[:, :], ACT.Copy, scale=UNW).then_inc(v_ready.sem, 1)

            def a_part(b, par, kind, n):
                cols = slice(P * n, P * n + P)
                if kind[-1] == "h":
                    return
                bank = work[BANK_A[kind, n]]
                if kind == "CT":
                    act.wait_ge(ctxT_ps.sem, ctxT_ps.at(b, n + 1))
                    act.activation(ctxT_hi[:, :, cols], bank[:, :].rearrange("p (t c) -> p t c", t=DT), ACT.Copy)\
                       .then_inc(ctxT_hi_s.sem, 1)
                if kind == "XT":
                    act.wait_ge(xT_ps.sem, xT_ps.at(b, n + 1))
                    act.activation(xT_hi[:, :, cols], bank[:, :].rearrange("p (t c) -> p t c", t=DT), ACT.Copy)\
                       .then_inc(xT_hi_s.sem, 1)
                if kind == "Q":
                    act.wait_ge(q_ps.sem, q_ps.at(b, n + 1))
                    act.activation(q_hi[:, n, :], bank[:, :], ACT.Identity, bias=bq_col[:, n:n + 1])\
                       .then_inc(q_hi_s.sem, 1)
                if kind == "V":
                    copy_v(b, par, n, bank)
                if kind == "K":
                    act.wait_ge(k_ps.sem, k_ps.at(b, n + 1))
                    act.activation(k_hi[:, n, :], bank[:, :], ACT.Identity, bias=bk_col[:, n:n + 1])\
                       .then_inc(k_hi_s.sem, 1)

            def normalise(b, buf, t, step_s, steps, ready):
                act.wait_ge(step_s.sem, step_s.at(b, steps))
                act.activation(xn[:, t, :], buf[:, t, :], ACT.Identity, bias=ln_tmp[:, 7, t:t + 1],
                               scale=ln_tmp[:, 6, t:t + 1]).then_inc(ready.sem, 1)

            def step(i, par, tables, with_d, with_b):
                def copy_o(g):
                    act.wait_ge(pv_done.sem, pv_done.at(i, TT * (g + 1)))
                    if g >= 1:
                        act.wait_ge(o_lo_s.sem, o_lo_s.at(i, g))
                    act.activation(o_buf[:, :], oT[:, :], ACT.Copy).then_inc(o_copied.sem, 1)

                def o_high(g):
                    act.wait_ge(o_scaled.sem, o_scaled.at(i, g + 1))
                    act.activation(o_hi[:, g, :], o_buf[:, :], ACT.Copy).then_inc(o_hi_s.sem, 1)

                for s in range(STEPS):
                    if with_b and s == 0:
                        for kind, n in A_AT[s]:
                            a_part(i + 1, 1 - par, kind, n)
                    if with_d:
                        for pr in range(2):
                            act.wait_ge(score_ps.sem, score_ps.at(i, 2 * s + pr + 1))
                            if s >= RING and pr == 0:
                                act.wait_ge(pv_done.sem, pv_done.at(i, s - RING + 1))
                                late = s - RING
                                adds = (TT - 1) * (late // TT) + max(late % TT, 1)
                                act.wait_ge(sum_pool.sem, sum_pool.at(i, adds))
                                act.wait_ge(sum_dve.sem, sum_dve.at(i, adds))
                            if s == 2 and pr == 0 and not (isinstance(i, int) and i == 0):
                                act.wait_ge(out_ready.sem, out_ready.at(i - 1, TT))
                            act.activation(probs[s % RING][:, 2 * pr:2 * pr + 2, :], scores[pr][:, :, :], ACT.Exp,
                                           scale=EXP_SCALE).then_inc(exp_done.sem, 1)
                    if with_b and s >= 1:
                        for kind, n in A_AT[s]:
                            a_part(i + 1, 1 - par, kind, n)
                    if not with_d and s in SPLIT_AT:
                        split_high(SPLIT_AT[s])
                    if with_d and s % TT == 0 and s >= TT:
                        copy_o(s // TT - 1)
                    if with_b:
                        for t in range(TT):
                            if s == NORM_AT[t]:
                                normalise(i + 1, x_buf[1 - par], t, ln1_step, LN_STEPS, xn_ready)
                    if with_d and s >= OHI_AT and (s - OHI_AT) % TT == 0:
                        o_high((s - OHI_AT) // TT)
                bank_of = tables[2]
                for kind, n in phase2(with_d, with_b):
                    bank = work[bank_of[kind, n]] if (kind, n) in bank_of else None
                    cols = slice(P * n, P * n + P)
                    if kind == "DEN":
                        copy_o(n)
                        o_high(n)
                    if kind == "V":
                        copy_v(i + 1, 1 - par, n, bank)
                    if kind == "PO" and n % 2:
                        for t in (n - 1, n):
                            normalise(i, x_buf[par], t, ln2_step, LN_STEPS * (n // 2 + 1), x1n_ready)
                    if kind == "T":
                        act.wait_ge(x1T_ps.sem, x1T_ps.at(i, n + 1))
                        act.activation(xT_hi[:, :, cols], bank[:, :].rearrange("p (t c) -> p t c", t=DT), ACT.Copy)\
                           .then_inc(x1T_hi_s.sem, 1)
                        if n >= 2:
                            act.wait_ge(x1T_lo_s.sem, x1T_lo_s.at(i, n - 1))
                        act.activation(x1T32[:, n % 2, :], bank[:, :], ACT.Copy).then_inc(x1T_copied.sem, 1)
                    if kind == "MT":
                        act.wait_ge(maxT_ps.sem, maxT_ps.at(i + 1, n + 1))
                        act.activation(max_rows[:, n, :], bank[:, :].bitcast(F16)[0:HEADS * TT // 2, 0:P], ACT.Copy)\
                           .then_inc(maxrow_s.sem, 1)
                    if kind == "LG":
                        act.wait_ge(gate_a.sem, gate_a.at(i, GATE_A))
                        act.activation(gate_exp[:, :, :], gap[:, :, :], ACT.Exp).then_inc(gate_exp_s.sem, 1)
                    if kind == "W1":
                        act.wait_ge(w1_ps.sem, w1_ps.at(i, n + 1))
                        act.activation(h_buf[:, n, :], bank[:, :], ACT.Gelu, scale=UNW).then_inc(h_ready.sem, 1)
                    if kind == "GT":
                        act.wait_ge(gateT_ps.sem, gateT_ps.at(i, 1))
                        act.activation(gateT[:, :], bank[:, :].bitcast(F16)[0:2 * EXPERTS, 0:T], ACT.Copy)\
                           .then_inc(gateT_s.sem, 1)
                    if kind == "W2":
                        act.wait_ge(w2_ps.sem, w2_ps.at(i, n + 1))
                        if n >= 2:
                            act.wait_ge(out_ready.sem, out_ready.at(i, n - 1))
                        act.activation(expert_out[:, n % 2, :], bank[:, :], ACT.Copy, scale=SCALING * UNW)\
                           .then_inc(w2_copied.sem, 1)
                    if kind == "GB":
                        act.wait_ge(gh32_s.sem, gh32_s.at(i, n + 1))
                        act.activation(gh_hi[:, n, :], gh32[:, n % 2, :], ACT.Copy).then_inc(gh_hi_s.sem, 1)
                        if n == DT - 1:
                            act.activation(table_probe[:, :], ones[:, 0:1], ACT.Exp)

            run_steps(act, step)

        @block.vector
        def _(dve):
            dve.memset(ones[:, :], 1.0).then_inc(ones_set.sem, 1)
            def split_low(n):
                name = weights[n][0]
                dve.wait_ge(setup_hi.sem, SETUP + n)
                dve.scalar_tensor_tensor(out=w_lo[name][:, :, :], in0=stage[n % STAGES], scalar=SCALE_W,
                                         in1=w_hi[name][:, :, :], op0=ALU.mult, op1=ALU.subtract)\
                   .then_inc(setup_lo.sem, 1)

            dve.wait_ge(const_in.sem, 9 * DMA)
            dve.tensor_scalar(bq_col[:, :], bq_col[:, :], SCALE_W, None, ALU.mult).then_inc(setup_lo.sem, 1)
            dve.tensor_scalar(bk_col[:, :], bk_col[:, :], SCALE_W, None, ALU.mult).then_inc(setup_lo.sem, 1)
            dve.wait_ge(setup_hi.sem, SETUP - 1)
            dve.scalar_tensor_tensor(out=wg_lo[:, :, :],
                                     in0=o_buf[:, 0:DT * EXPERTS].rearrange("p (t e) -> p t e", t=DT),
                                     scalar=SCALE_W, in1=wg_hi[:, :, :], op0=ALU.mult, op1=ALU.subtract)\
               .then_inc(setup_lo.sem, 1)
            dve.tensor_tensor(bv_lo[:, :], bv_col[:, :], bv_hi[:, :], ALU.subtract).then_inc(setup_lo.sem, 1)
            split_low(0)

            def moments(tiles, stats_s, moment_s, b, base):
                c = slice(tiles[0], tiles[-1] + 1)
                mean_a, m2_a, mean_b, m2_b = (stats[:, c, n] for n in (1, 2, 4, 5))
                diff, m2, sq, quarter = (moment_tmp[:, n, c] for n in range(4))
                dve.wait_ge(stats_s.sem, stats_s.at(b, tiles[-1] + 1))
                dve.tensor_tensor(ln_tmp[:, 0, c], mean_a, mean_b, ALU.add).then_inc(moment_s.sem, 1)
                dve.tensor_tensor(diff, mean_a, mean_b, ALU.subtract).then_inc(moment_s.sem, 1)
                dve.tensor_tensor(m2, m2_a, m2_b, ALU.add).then_inc(moment_s.sem, 1)
                dve.wait_ge(moment_s.sem, moment_s.at(b, base + 2))
                dve.tensor_tensor(sq, diff, diff, ALU.mult).then_inc(moment_s.sem, 1)
                dve.wait_ge(moment_s.sem, moment_s.at(b, base + 4))
                dve.tensor_scalar(quarter, sq, 0.25, LN_EPS, ALU.mult, ALU.add).then_inc(moment_s.sem, 1)
                dve.wait_ge(moment_s.sem, moment_s.at(b, base + 5))
                dve.scalar_tensor_tensor(out=ln_tmp[:, 1, c], in0=m2, scalar=1.0 / D, in1=quarter,
                                         op0=ALU.mult, op1=ALU.add).then_inc(moment_s.sem, 1)

            def a_part(b, kind, n):
                cols = slice(P * n, P * n + P)
                if kind[-1] == "h":
                    return
                bank = work[BANK_A[kind, n]]
                tiles = bank[:, :].rearrange("p (t c) -> p t c", t=DT)
                if kind == "CT":
                    dve.wait_ge(ctxT_hi_s.sem, ctxT_hi_s.at(b, n + 1))
                    dve.tensor_tensor(ctxT_lo[:, :, cols], tiles, ctxT_hi[:, :, cols], ALU.subtract)\
                       .then_inc(ctxT_lo_s.sem, 1)
                if kind == "XT":
                    dve.wait_ge(xT_hi_s.sem, xT_hi_s.at(b, n + 1))
                    dve.tensor_tensor(xT_lo[:, :, cols], tiles, xT_hi[:, :, cols], ALU.subtract)\
                       .then_inc(xT_lo_s.sem, 1)
                if kind == "Q":
                    dve.wait_ge(q_hi_s.sem, q_hi_s.at(b, n + 1))
                    dve.scalar_tensor_tensor(out=q_lo[:, n, :], in0=bank[:, :], scalar=bq_col[:, n:n + 1],
                                             in1=q_hi[:, n, :], op0=ALU.add, op1=ALU.subtract)\
                       .then_inc(q_lo_s.sem, 1)
                if kind == "K":
                    dve.wait_ge(k_hi_s.sem, k_hi_s.at(b, n + 1))
                    dve.scalar_tensor_tensor(out=k_lo[:, n, :], in0=bank[:, :], scalar=bk_col[:, n:n + 1],
                                             in1=k_hi[:, n, :], op0=ALU.add, op1=ALU.subtract)\
                       .then_inc(k_lo_s.sem, 1)

            def step(i, par, tables, with_d, with_b):
                def scale_o(g):
                    dve.wait_ge(den_ps.sem, den_ps.at(i, g + 1))
                    if g >= 1:
                        dve.wait_ge(o_scaled.sem, o_scaled.at(i, g))
                    dve.reciprocal(inv_den[:, :], den[:, :]).then_inc(inv_ready.sem, 1)
                    dve.wait_ge(inv_ready.sem, inv_ready.at(i, g + 1))
                    dve.wait_ge(o_copied.sem, o_copied.at(i, g + 1))
                    dve.tensor_tensor(o_buf[:, :], o_buf[:, :], inv_den[:, :], ALU.mult).then_inc(o_scaled.sem, 1)

                for s in range(STEPS):
                    if with_b:
                        for kind, n in A_AT[s]:
                            a_part(i + 1, kind, n)
                        if not with_d and s in SPLIT_AT:
                            split_low(SPLIT_AT[s])
                        if s == STATS_AT:
                            dve.wait_ge(x_in.sem, x_in.at(i + 1, DMA))
                            for t in range(TT):
                                dve.bn_stats(stats[:, t, :], x_buf[1 - par][:, t, :]).then_inc(stats1.sem, 1)
                            moments(range(TT), stats1, moments1, i + 1, 0)
                    if with_d and s % TT and s < STEPS - 1:
                        add_probs(dve, i, s, slice(HT // 2, HT), sum_dve)
                    if with_d and s >= DEN_AT and (s - DEN_AT) % TT == 0:
                        scale_o((s - DEN_AT) // TT)
                if not with_d:
                    dve.wait_ge(bo_ps.sem, 1)
                    dve.scalar_tensor_tensor(out=bo_row[:, :], in0=work[2][:, :], scalar=UNW, in1=bo_row[:, :],
                                             op0=ALU.mult, op1=ALU.add).then_inc(bo_ready.sem, 1)
                bank_of = tables[2]
                for kind, n in phase2(with_d, with_b):
                    bank = work[bank_of[kind, n]] if (kind, n) in bank_of else None
                    if kind == "B":
                        dve.wait_ge(max_ps.sem, max_ps.at(i + 1, n + 1))
                        dve.tensor_reduce(maxima[:, 2 * n:2 * n + 2], scores[n % 2][:, :, :], AX_X, ALU.max)\
                           .then_inc(max_done.sem, 1)
                        if n % (MAX_UNITS // 2) == MAX_UNITS // 2 - 1:
                            half = n // (MAX_UNITS // 2)
                            c = slice(MAX_UNITS * half, MAX_UNITS * (half + 1))
                            dve.wait_ge(max_done.sem, max_done.at(i + 1, n + 1))
                            dve.tensor_scalar(neg_max[:, c], maxima[:, c], -1.0 / MAX_UNIT, None, ALU.mult)\
                               .then_inc(negmax_s.sem, 1)
                    if kind == "DEN":
                        scale_o(n)
                    if kind == "PO":
                        dve.wait_ge(op_ps.sem, op_ps.at(i, n + 1))
                        dve.wait_ge(xbo_ready.sem, xbo_ready.at(i, n + 1))
                        dve.scalar_tensor_tensor(out=x_buf[par][:, n, :], in0=bank[:, :], scalar=UNW,
                                                 in1=x_buf[par][:, n, :], op0=ALU.mult, op1=ALU.add)\
                           .then_inc(x1_ready.sem, 1)
                        dve.wait_ge(x1_ready.sem, x1_ready.at(i, n + 1))
                        dve.bn_stats(stats[:, n, :], x_buf[par][:, n, :]).then_inc(stats2.sem, 1)
                        if n % 2:
                            moments(range(n - 1, n + 1), stats2, moments2, i, MOMENTS * (n // 2))
                    if kind == "LG":
                        dve.wait_ge(logit_ps.sem, logit_ps.at(i, 1))
                        dve.scalar_tensor_tensor(
                            out=logits[:, :, :],
                            in0=bank[:, 0:TT * EXPERTS].rearrange("p (t e) -> p t e", t=TT), scalar=UNW,
                            in1=bg_row[:, :].unsqueeze(1).to_broadcast([P, TT, EXPERTS]),
                            op0=ALU.mult, op1=ALU.add).then_inc(gate_a.sem, 1)
                        dve.wait_ge(gate_a.sem, gate_a.at(i, 1))
                        other = logits[:, :, :].unsqueeze(2).to_broadcast([P, TT, EXPERTS, EXPERTS])
                        own = logits[:, :, :].unsqueeze(3).to_broadcast([P, TT, EXPERTS, EXPERTS])
                        tri = lower_tri[:, :, :].unsqueeze(1).to_broadcast([P, TT, EXPERTS, EXPERTS])
                        dve.tensor_reduce(top1[:, :], logits[:, :, :], AX_X, ALU.max).then_inc(gate_a.sem, 1)
                        dve.tensor_tensor(cmp_gt, other, own, ALU.is_gt).then_inc(gate_a.sem, 1)
                        dve.tensor_tensor(cmp_eq, other, own, ALU.is_equal).then_inc(gate_a.sem, 1)
                        dve.wait_ge(gate_a.sem, gate_a.at(i, 4))
                        dve.tensor_tensor(cmp_eq, cmp_eq, tri, ALU.mult).then_inc(gate_a.sem, 1)
                        dve.wait_ge(gate_a.sem, gate_a.at(i, 5))
                        dve.tensor_tensor(cmp_gt, cmp_gt, cmp_eq, ALU.add).then_inc(gate_a.sem, 1)
                        dve.wait_ge(gate_a.sem, gate_a.at(i, 6))
                        dve.tensor_reduce(rank[:, :, :], cmp_gt, AX_X, ALU.add).then_inc(gate_a.sem, 1)
                        dve.tensor_tensor(gap[:, :, :], logits[:, :, :],
                                          top1[:, :].unsqueeze(2).to_broadcast([P, TT, EXPERTS]),
                                          ALU.subtract).then_inc(gate_a.sem, 1)
                    if (kind, n) == ("W1", 1):
                        dve.wait_ge(gate_a.sem, gate_a.at(i, GATE_A))
                        dve.wait_ge(gate_exp_s.sem, gate_exp_s.at(i, 1))
                        dve.scalar_tensor_tensor(out=gates[:, :, :], in0=rank[:, :, :], scalar=2.0,
                                                 in1=gate_exp[:, :, :], op0=ALU.is_lt, op1=ALU.mult)\
                           .then_inc(gate_b.sem, 1)
                        dve.wait_ge(gate_b.sem, gate_b.at(i, 1))
                        dve.tensor_reduce(gate_den[:, 0, :], gates[:, :, :], AX_X, ALU.add).then_inc(gate_b.sem, 1)
                        dve.wait_ge(gate_b.sem, gate_b.at(i, 2))
                        dve.reciprocal(gate_den[:, 1, :], gate_den[:, 0, :]).then_inc(gate_b.sem, 1)
                        dve.wait_ge(gate_b.sem, gate_b.at(i, 3))
                        dve.tensor_tensor(gates[:, :, :], gates[:, :, :],
                                          gate_den[:, 1, :].unsqueeze(2).to_broadcast([P, TT, EXPERTS]),
                                          ALU.mult).then_inc(gate_b.sem, 1)
                        dve.wait_ge(gate_b.sem, gate_b.at(i, 4))
                        dve.tensor_copy(gate_pair[:, :, 0:EXPERTS], gates[:, :, :]).then_inc(gate_b.sem, 1)
                        dve.wait_ge(gate_b.sem, gate_b.at(i, 5))
                        dve.tensor_tensor(gate_pair[:, :, EXPERTS:2 * EXPERTS], gates[:, :, :],
                                          gate_pair[:, :, 0:EXPERTS], ALU.subtract).then_inc(gate_b.sem, 1)
                    if kind == "GB":
                        dve.wait_ge(gbc_ps.sem, gbc_ps.at(i, n + 1))
                        dve.wait_ge(h_ready.sem, h_ready.at(i, n + 1))
                        if n >= 2:
                            dve.wait_ge(gh_lo_s.sem, gh_lo_s.at(i, n - 1))
                        dve.tensor_tensor(gh32[:, n % 2, :], bank[:, :], h_buf[:, n, :], ALU.mult)\
                           .then_inc(gh32_s.sem, 1)

            run_steps(dve, step)

        @block.tensor
        def _(pe):
            pe.wait_ge(const_in.sem, 9 * DMA)

            def three(dst, lhs_hi, lhs_lo, rhs_hi, rhs_lo, tiles=range(DT), of=DT):
                for t in tiles:
                    pe.matmul(dst, lhs_hi(t), rhs_hi(t), start=(t == 0), stop=False)
                    pe.matmul(dst, lhs_hi(t), rhs_lo(t), start=False, stop=False)
                    last = pe.matmul(dst, lhs_lo(t), rhs_hi(t), start=False, stop=(t == of - 1))
                return last

            def halves(kind, n, order, done, *operands):
                name = kind.rstrip("h")
                split = (name + "h", n) in order
                tiles = range(DT // 2) if kind != name else range(DT // 2, DT) if split else range(DT)
                last = three(*operands, tiles)
                if kind == name:
                    last.then_inc(done.sem, 1)

            def project_v(kind, n, bank, order):
                cols = slice(P * n, P * n + P)
                halves(kind, n, order, v_ps, bank[:, :], lambda t: ctxT_hi[:, t, cols],
                       lambda t: ctxT_lo[:, t, cols], lambda t: w_hi["v"][:, t, :], lambda t: w_lo["v"][:, t, :])

            def free(i, prior):
                if prior is None:
                    return
                kind, n, offset = prior
                sem = bank_read[kind]
                pe.wait_ge(sem.sem, sem.at(i + offset, n + 1))

            def a_part(i, kind, n, prior):
                b = i + 1
                name = kind.rstrip("h")
                if kind != name or (name + "h", n) not in A_ORDER:
                    free(i, prior[name, n])
                bank = work[BANK_A[name, n]]
                cols = slice(P * n, P * n + P)
                if kind == "CT":
                    if n == 0:
                        pe.wait_ge(ctx_in.sem, ctx_in.at(b, DMA))
                    for t in range(DT):
                        last = pe.transpose(bank[:, P * t:P * t + P], ctx_buf[:, n, P * t:P * t + P], ident32[:, :])
                    last.then_inc(ctxT_ps.sem, 1)
                if kind == "XT":
                    pe.wait_ge(xn_ready.sem, xn_ready.at(b, n + 1))
                    for t in range(DT):
                        last = pe.transpose(bank[:, P * t:P * t + P], xn[:, n, P * t:P * t + P], ident32[:, :])
                    last.then_inc(xT_ps.sem, 1)
                if name == "Q":
                    if n == 0 and prior is PROLOGUE[0]:
                        pe.wait_ge(setup_lo.sem, SETUP + 1)
                    if n == 0:
                        pe.wait_ge(xT_lo_s.sem, xT_lo_s.at(b, TT))
                    halves(kind, n, A_ORDER, q_ps, bank[:, :], lambda t: w_hi["q"][:, t, cols],
                           lambda t: w_lo["q"][:, t, cols], lambda t: xT_hi[:, t, :], lambda t: xT_lo[:, t, :])
                if name == "K":
                    if n == 0 and prior is PROLOGUE[0]:
                        pe.wait_ge(setup_lo.sem, SETUP)
                    if n == 0:
                        pe.wait_ge(ctxT_lo_s.sem, ctxT_lo_s.at(b, TT))
                    halves(kind, n, A_ORDER, k_ps, bank[:, :], lambda t: w_hi["k"][:, t, cols],
                           lambda t: w_lo["k"][:, t, cols], lambda t: ctxT_hi[:, t, :], lambda t: ctxT_lo[:, t, :])
                if name == "V":
                    project_v(kind, n, bank, A_ORDER)

            def step(i, par, tables, with_d, with_b):
                prior_a, (oT_prior, den_prior), bank_of, prior_d, _ = tables

                def score_step(s):
                    g, kt = s // TT, s % TT
                    if s == 0:
                        pe.wait_ge(maxrow_in[0].sem, maxrow_in[0].at(i, DMA))
                    if s == STEPS // 2:
                        pe.wait_ge(maxrow_in[1].sem, maxrow_in[1].at(i, DMA))
                    for pr in range(2):
                        if s >= 1:
                            pe.wait_ge(exp_done.sem, exp_done.at(i, 2 * s - 1 + pr))
                        else:
                            pe.wait_ge(max_done.sem, max_done.at(i, MAX_UNITS - 1 + pr))
                        for j in range(2):
                            h = HT * g + 2 * pr + j
                            last = pe.matmul(scores[pr][:, j, :], k_stack[0:STACK + 1, h, P * kt:P * kt + P],
                                             q_stack[0:STACK + 1, h, :], start=True, stop=True)
                        last.then_inc(score_ps.sem, 1)

                def values_step(s):
                    g, kt = s // TT, s % TT
                    if s == 0:
                        free(i, oT_prior)
                        pe.wait_ge(v_ready.sem, v_ready.at(i, TT))
                    elif kt == 0:
                        pe.wait_ge(o_copied.sem, o_copied.at(i, g))
                    pe.wait_ge(exp_done.sem, exp_done.at(i, 2 * s + 2))
                    for j in range(HT):
                        h = HT * g + j
                        last = pe.matmul(oT[DK * j:DK * j + DK, :], v_buf[par][:, kt, DK * h:DK * h + DK],
                                         probs[s % RING][:, j, :], start=(kt == 0), stop=(kt == TT - 1))
                    last.then_inc(pv_done.sem, 1)

                def denominators(g):
                    if g == 0:
                        free(i, den_prior)
                    else:
                        pe.wait_ge(inv_ready.sem, inv_ready.at(i, g))
                    adds = min((TT - 1) * (g + 1), SUMS)
                    pe.wait_ge(sum_pool.sem, sum_pool.at(i, adds))
                    pe.wait_ge(sum_dve.sem, sum_dve.at(i, adds))
                    for j in range(HT):
                        parts = [prob_sum] if g < GROUPS - 1 else [prob_sum, probs[(STEPS - 1) % RING]]
                        for part in parts:
                            last = pe.matmul(den[DK * j:DK * j + DK, :], ones[:, :], part[:, j, :],
                                             start=part is parts[0], stop=part is parts[-1])
                    last.then_inc(den_ps.sem, 1)

                for s in range(STEPS):
                    if with_d and s >= 1:
                        score_step(s)
                    if with_b:
                        for kind, n in A_AT[s]:
                            a_part(i, kind, n, prior_a)
                    if with_d and s == 0:
                        score_step(s)
                    if with_d and s >= 1:
                        values_step(s - 1)
                    if with_d and s >= DEN_AT and (s - DEN_AT) % TT == 0:
                        denominators((s - DEN_AT) // TT)
                if with_d:
                    values_step(STEPS - 1)

                if not with_d:
                    pe.wait_ge(ln_const.sem, 3)
                    pe.wait_ge(ones_set.sem, 1)
                    pe.wait_ge(setup_lo.sem, SETUP + len(weights) - 1)
                    three(work[2][:, :], lambda t: bv_hi[:, t:t + 1].to_broadcast([P, P]),
                          lambda t: bv_lo[:, t:t + 1].to_broadcast([P, P]),
                          lambda t: w_hi["o"][:, t, :], lambda t: w_lo["o"][:, t, :]).then_inc(bo_ps.sem, 1)
                    pe.wait_ge(bo_ready.sem, 1)
                order = phase2(with_d, with_b)
                for kind, n in order:
                    if kind == "B":
                        h, qt = n // 2, 2 * (n % 2)
                        if n == 0:
                            pe.wait_ge(stack_in[0].sem, stack_in[0].at(i + 1, 24 * DMA))
                            if with_d:
                                pe.wait_ge(exp_done.sem, exp_done.at(i, 2 * STEPS))
                        if n == MAX_UNITS // 2:
                            pe.wait_ge(stack_in[1].sem, stack_in[1].at(i + 1, 24 * DMA))
                        if n >= 2:
                            pe.wait_ge(max_done.sem, max_done.at(i + 1, n - 1))
                        for j in range(2):
                            q = P * (qt + j)
                            last = pe.matmul(scores[n % 2][:, j, :], q_stack[0:STACK, h, q:q + P],
                                             k_stack[0:STACK, h, :], start=True, stop=True)
                        last.then_inc(max_ps.sem, 1)
                        continue
                    if kind == "DEN":
                        denominators(n)
                    if kind == "DEN":
                        continue
                    name = kind.rstrip("h")
                    if kind != "PO" and (kind != name or (name + "h", n) not in order):
                        free(i, prior_d[name, n])
                    bank = work[bank_of[name, n]]
                    cols = slice(P * n, P * n + P)
                    if kind == "MT":
                        pe.wait_ge(negmax_s.sem, negmax_s.at(i + 1, n + 1))
                        pe.transpose(bank[:, :].bitcast(F16)[0:MAX_UNITS, 0:P],
                                     neg_max[:, MAX_UNITS * n:MAX_UNITS * (n + 1)], ident16[:, :])\
                          .then_inc(maxT_ps.sem, 1)
                    if kind in ("OP", "PO"):
                        if n == 0:
                            pe.wait_ge(o_lo_s.sem, o_lo_s.at(i, GROUPS if kind == "PO" else GROUPS - 1))
                        last = three(bank[:, :], lambda t: o_hi[:, t, cols], lambda t: o_lo[:, t, cols],
                                     lambda t: w_hi["o"][:, t, :], lambda t: w_lo["o"][:, t, :],
                                     range(GROUPS - 1, GROUPS) if kind == "PO" else range(GROUPS - 1), GROUPS)
                        if kind == "PO":
                            last.then_inc(op_ps.sem, 1)
                    if name == "V":
                        project_v(kind, n, bank, order)
                    if kind == "T":
                        pe.wait_ge(x1n_ready.sem, x1n_ready.at(i, n + 1))
                        for t in range(DT):
                            last = pe.transpose(bank[:, P * t:P * t + P], xn[:, n, P * t:P * t + P], ident32[:, :])
                        last.then_inc(x1T_ps.sem, 1)
                    if kind == "LG":
                        pe.wait_ge(x1T_lo_s.sem, x1T_lo_s.at(i, TT))
                        for m in range(TT):
                            tok = slice(P * m, P * m + P)
                            last = three(bank[:, EXPERTS * m:EXPERTS * (m + 1)],
                                         lambda t: xT_hi[:, t, tok], lambda t: xT_lo[:, t, tok],
                                         lambda t: wg_hi[:, t, :], lambda t: wg_lo[:, t, :])
                        last.then_inc(logit_ps.sem, 1)
                    if name == "W1":
                        halves(kind, n, order, w1_ps, bank[:, :], lambda t: w_hi["1"][:, t, cols],
                               lambda t: w_lo["1"][:, t, cols], lambda t: xT_hi[:, t, :], lambda t: xT_lo[:, t, :])
                    if kind == "GT":
                        pe.wait_ge(gate_b.sem, gate_b.at(i, GATE_B))
                        for m in range(TT):
                            last = pe.transpose(bank[:, :].bitcast(F16)[0:2 * EXPERTS, P * m:P * m + P],
                                                gate_pair[:, m, :], ident16[:, :])
                        last.then_inc(gateT_ps.sem, 1)
                    if kind == "GB":
                        if n == 0:
                            pe.wait_ge(gateT_s.sem, gateT_s.at(i, 1))
                        pe.matmul(bank[:, :], select16[:, n, :], gateT[:, :], start=True, stop=True)\
                          .then_inc(gbc_ps.sem, 1)
                    if name == "W2":
                        pe.wait_ge(gh_lo_s.sem, gh_lo_s.at(i, DT // 2 if kind != name else DT))
                        halves(kind, n, order, w2_ps, bank[:, :], lambda t: gh_hi[:, t, cols],
                               lambda t: gh_lo[:, t, cols], lambda t: w_hi["2"][:, t, :], lambda t: w_lo["2"][:, t, :])

            run_steps(pe, step)


def kernel(**inputs):
    import concourse.bacc as _bacc
    from concourse.bass_utils import run_bass_kernel_spmd as _run

    def flip(name):
        a = np.asarray(inputs[name])
        return np.ascontiguousarray(a.reshape(-1, a.shape[-1]).T)

    def by_partition(name):
        return np.ascontiguousarray(np.asarray(inputs[name]).reshape(-1, P).T)

    w2 = np.asarray(inputs["L0_ffn_W2"])
    experts = w2.shape[0]
    er = experts * w2.shape[2]
    select = np.zeros((2 * experts, er), np.float32)
    for e in range(experts):
        select[[e, experts + e], e * (er // experts):(e + 1) * (er // experts)] = 1.0
    arrays = {
        "x": inputs["x"], "ctx": inputs["ctx_1024"],
        "wq_t": flip("L0_xattn_Wq"), "bq": by_partition("L0_xattn_bq"),
        "wk_t": flip("L0_xattn_Wk"), "bk": by_partition("L0_xattn_bk"),
        "wv_t": flip("L0_xattn_Wv"), "bv": by_partition("L0_xattn_bv"),
        "wo_t": flip("L0_xattn_Wo"), "bo": inputs["L0_xattn_bo"],
        "wg_t": flip("L0_ffn_Wg"), "bg": inputs["L0_ffn_bg"],
        "w1_t": flip("L0_ffn_W1"),
        "w2_t": np.ascontiguousarray(w2.transpose(0, 2, 1).reshape(er, w2.shape[1])),
        "ident": np.eye(P, dtype=np.float32), "select": select,
        "lower": np.tril(np.ones((experts, experts), np.float32), -1),
    }
    arrays = {n: np.ascontiguousarray(a) for n, a in arrays.items()}
    nc = _bacc.Bacc("TRN2", target_bir_lowering=False, num_devices=1, dynamic_dma_scratch_size=4096)
    args = [nc.dram_tensor(n, a.shape, mybir.dt.from_np(a.dtype), kind="ExternalInput").ap()
            for n, a in arrays.items()]
    out = nc.dram_tensor("out", arrays["x"].shape, F32, kind="ExternalOutput").ap()
    xattn_moe_kernel(nc, *args, out)
    r = _run(nc, [arrays], core_ids=[0])
    return r.results[0]["out"]
```
